# Optimizing a Trainium2 kernel written in Bass

```python
import numpy as np
import jax
import jax.numpy as jnp

def _softmax(x, axis=-1):
    return jax.nn.softmax(x, axis=axis)

def _gelu(x):
    return jax.nn.gelu(x, approximate=True)

def _silu(x):
    return jax.nn.silu(x)

def _sigmoid(x):
    return jax.nn.sigmoid(x)

def _layernorm(x, axis=-1, eps=1e-05):
    m = jnp.mean(x, axis=axis, keepdims=True)
    v = jnp.var(x, axis=axis, keepdims=True)
    return (x - m) / jnp.sqrt(v + eps)

def _scatter_add(tgt, idx, src, axis=0):
    return tgt.at[idx].add(src)

def _segment_sum(src, seg, n):
    return jax.ops.segment_sum(src, seg, n)
kernel_name = 'mk_xattn_seq_d1_seqx_r8_d39492'

def setup_inputs(seed: int=0):
    np.random.seed(seed)
    _w = jnp.asarray

    def _rec_inputs():
        import jax
        import jax.numpy as jnp
        _rk = jax.random.key(seed)
        x = 7.22e-05 + 1 * jax.random.normal(jax.random.fold_in(_rk, 1), (4, 256, 256), jnp.float32)
        _lenS = 256 - jax.random.randint(jax.random.fold_in(_rk, 7), (4,), 0, max(1, 256 // 4) + 1, jnp.int32)
        _lenS2 = 256 - jax.random.randint(jax.random.fold_in(_rk, 8), (4,), 0, max(1, 256 // 4) + 1, jnp.int32)
        _ctx_2048P = jax.random.normal(jax.random.fold_in(_rk, 11), (4, 16, 256), jnp.float32)
        _ctx_2048c = jax.random.dirichlet(jax.random.fold_in(_rk, 511), 0.3 * jnp.ones((16,), jnp.float32), (4, 256))
        _ctx_2048t = jnp.einsum('bsk,bkd->bsd', _ctx_2048c, _ctx_2048P)
        _ctx_2048t = _ctx_2048t * jax.lax.rsqrt(jnp.mean(jnp.square(_ctx_2048t)) + 1e-12) * 0.953939
        ctx_2048 = 0.000189249 + 0.0999589 * (_ctx_2048t + 0.3 * jax.random.normal(jax.random.fold_in(_rk, 611), (4, 256, 256), jnp.float32))
        return (x, ctx_2048)
    x, ctx_2048 = _rec_inputs()

    def _L0_xattn_setup():
        import jax, jax.numpy as jnp
        import numpy as np
        E, H, L, B = (256, 32, 128, 4)
        S = E // H
        DM, DD = (32, 64)

        def _ln(x, w, b, eps=1e-05):
            m = x.mean(-1, keepdims=True)
            v = ((x - m) ** 2).mean(-1, keepdims=True)
            return (x - m) / jnp.sqrt(v + eps) * w + b

        def _block(x, state, ln1_w, ln1_b, ln2_w, ln2_b, maa_x, maa_w1, maa_w2, maa_stack, time_decay, td_w1, td_w2, u, Wr, Wk, Wv, Wg, Wo, gn_w, gn_b, ffn_maa_k, ffn_maa_r, Wfk, Wfr, Wfv):
            b, l, e = x.shape
            h = u.shape[0]
            s_ = e // h
            xa = _ln(x, ln1_w, ln1_b)
            sx = jnp.concatenate([state[:, 1:2] - xa[:, :1], xa[:, :-1] - xa[:, 1:]], axis=1)
            xxx = jnp.tanh((xa + sx * maa_x) @ maa_w1).reshape(b, l, 5, DM)
            xxx = jnp.einsum('blfd,fde->blfe', xxx, maa_w2)
            xm = xa[:, :, None] + sx[:, :, None] * (maa_stack + xxx)
            xk, xw, xv, xr, xg = (xm[:, :, j] for j in range(5))
            w = jnp.exp(-jnp.exp(time_decay + jnp.tanh(xw @ td_w1) @ td_w2)).reshape(b, l, h, s_)
            r = (xr @ Wr.T).reshape(b, l, h, s_)
            k = (xk @ Wk.T).reshape(b, l, h, s_)
            v = (xv @ Wv.T).reshape(b, l, h, s_)
            g = jax.nn.silu(xg @ Wg.T)
            s0 = state[:, 2:2 + s_].reshape(b, h, s_, s_)

            def step(s, rkvw):
                r_t, k_t, v_t, w_t = rkvw
                a = k_t[..., :, None] * v_t[..., None, :]
                out = jnp.einsum('bhi,bhij->bhj', r_t, u * a + s)
                s = a + w_t[..., :, None] * s
                return (s, out)
            rkvw = tuple((jnp.moveaxis(t, 1, 0) for t in (r, k, v, w)))
            _, out = jax.lax.scan(step, s0, rkvw)
            out = jnp.moveaxis(out, 0, 1).reshape(b, l, e)
            og = out.reshape(b, l, h, s_)
            m = og.mean(-1, keepdims=True)
            va = ((og - m) ** 2).mean(-1, keepdims=True)
            og = ((og - m) / jnp.sqrt(va + 1e-05)).reshape(b, l, e) * gn_w + gn_b
            x1 = x + og * g @ Wo.T
            xc = _ln(x1, ln2_w, ln2_b)
            sx2 = jnp.concatenate([state[:, 0:1] - xc[:, :1], xc[:, :-1] - xc[:, 1:]], axis=1)
            xk2 = xc + sx2 * ffn_maa_k
            xr2 = xc + sx2 * ffn_maa_r
            rr = jax.nn.sigmoid(xr2 @ Wfr.T)
            kk = jnp.square(jax.nn.relu(xk2 @ Wfk.T))
            return x1 + rr * (kk @ Wfv.T)
        key = jax.random.key(seed)
        ks = jax.random.split(key, 24)
        sc = 0.02
        d = {'x': jax.random.normal(ks[0], (B, L, E), jnp.float32), 'state': jax.random.normal(ks[1], (B, 2 + S, E), jnp.float32) * 0.1, 'ln1_w': jnp.ones((E,), jnp.float32), 'ln1_b': jnp.zeros((E,), jnp.float32), 'ln2_w': jnp.ones((E,), jnp.float32), 'ln2_b': jnp.zeros((E,), jnp.float32), 'maa_x': jax.random.normal(ks[2], (E,), jnp.float32) * 0.1, 'maa_w1': jax.random.normal(ks[3], (E, 5 * DM), jnp.float32) * sc, 'maa_w2': jax.random.normal(ks[4], (5, DM, E), jnp.float32) * sc, 'maa_stack': jax.random.normal(ks[5], (1, 5, E), jnp.float32) * 0.1, 'time_decay': jax.random.normal(ks[6], (E,), jnp.float32) * 0.5, 'td_w1': jax.random.normal(ks[7], (E, DD), jnp.float32) * sc, 'td_w2': jax.random.normal(ks[8], (DD, E), jnp.float32) * sc, 'u': jax.random.normal(ks[9], (H, S, 1), jnp.float32) * 0.1, 'Wr': jax.random.normal(ks[10], (E, E), jnp.float32) * sc, 'Wk': jax.random.normal(ks[11], (E, E), jnp.float32) * sc, 'Wv': jax.random.normal(ks[12], (E, E), jnp.float32) * sc, 'Wg': jax.random.normal(ks[13], (E, E), jnp.float32) * sc, 'Wo': jax.random.normal(ks[14], (E, E), jnp.float32) * sc, 'gn_w': jnp.ones((E,), jnp.float32), 'gn_b': jnp.zeros((E,), jnp.float32), 'ffn_maa_k': jax.random.normal(ks[15], (E,), jnp.float32) * 0.1, 'ffn_maa_r': jax.random.normal(ks[16], (E,), jnp.float32) * 0.1, 'Wfk': jax.random.normal(ks[17], (E, E), jnp.float32) * sc, 'Wfr': jax.random.normal(ks[18], (E, E), jnp.float32) * sc, 'Wfv': jax.random.normal(ks[19], (E, E), jnp.float32) * sc}
        return d
    _L0_xattn_all = _L0_xattn_setup()
    _L0_xattn_in = {k: v for k, v in _L0_xattn_all.items() if k in ('ln1_w', 'ln1_b', 'ln2_w', 'ln2_b', 'maa_x', 'maa_w1', 'maa_w2', 'maa_stack', 'time_decay', 'td_w1', 'td_w2', 'u', 'Wr', 'Wk', 'Wv', 'Wg', 'Wo', 'gn_w', 'gn_b', 'ffn_maa_k', 'ffn_maa_r', 'Wfk', 'Wfr', 'Wfv')}
    del _L0_xattn_all
    return {'x': x, 'ctx_2048': ctx_2048, 'L0_xattn_ln1_w': _L0_xattn_in['ln1_w'], 'L0_xattn_ln1_b': _L0_xattn_in['ln1_b'], 'L0_xattn_ln2_w': _L0_xattn_in['ln2_w'], 'L0_xattn_ln2_b': _L0_xattn_in['ln2_b'], 'L0_xattn_maa_x': _L0_xattn_in['maa_x'], 'L0_xattn_maa_w1': _L0_xattn_in['maa_w1'], 'L0_xattn_maa_w2': _L0_xattn_in['maa_w2'], 'L0_xattn_maa_stack': _L0_xattn_in['maa_stack'], 'L0_xattn_time_decay': _L0_xattn_in['time_decay'], 'L0_xattn_td_w1': _L0_xattn_in['td_w1'], 'L0_xattn_td_w2': _L0_xattn_in['td_w2'], 'L0_xattn_u': _L0_xattn_in['u'], 'L0_xattn_Wr': _L0_xattn_in['Wr'], 'L0_xattn_Wk': _L0_xattn_in['Wk'], 'L0_xattn_Wv': _L0_xattn_in['Wv'], 'L0_xattn_Wg': _L0_xattn_in['Wg'], 'L0_xattn_Wo': _L0_xattn_in['Wo'], 'L0_xattn_gn_w': _L0_xattn_in['gn_w'], 'L0_xattn_gn_b': _L0_xattn_in['gn_b'], 'L0_xattn_ffn_maa_k': _L0_xattn_in['ffn_maa_k'], 'L0_xattn_ffn_maa_r': _L0_xattn_in['ffn_maa_r'], 'L0_xattn_Wfk': _L0_xattn_in['Wfk'], 'L0_xattn_Wfr': _L0_xattn_in['Wfr'], 'L0_xattn_Wfv': _L0_xattn_in['Wfv']}

def reference(x, ctx_2048, L0_xattn_ln1_w, L0_xattn_ln1_b, L0_xattn_ln2_w, L0_xattn_ln2_b, L0_xattn_maa_x, L0_xattn_maa_w1, L0_xattn_maa_w2, L0_xattn_maa_stack, L0_xattn_time_decay, L0_xattn_td_w1, L0_xattn_td_w2, L0_xattn_u, L0_xattn_Wr, L0_xattn_Wk, L0_xattn_Wv, L0_xattn_Wg, L0_xattn_Wo, L0_xattn_gn_w, L0_xattn_gn_b, L0_xattn_ffn_maa_k, L0_xattn_ffn_maa_r, L0_xattn_Wfk, L0_xattn_Wfr, L0_xattn_Wfv):
    import jax
    import jax.numpy as jnp

    def _L0_xattn_ref(x, state, ln1_w, ln1_b, ln2_w, ln2_b, maa_x, maa_w1, maa_w2, maa_stack, time_decay, td_w1, td_w2, u, Wr, Wk, Wv, Wg, Wo, gn_w, gn_b, ffn_maa_k, ffn_maa_r, Wfk, Wfr, Wfv):
        import jax, jax.numpy as jnp
        import numpy as np
        E, H, L, B = (256, 32, 128, 4)
        S = E // H
        DM, DD = (32, 64)

        def _ln(x, w, b, eps=1e-05):
            m = x.mean(-1, keepdims=True)
            v = ((x - m) ** 2).mean(-1, keepdims=True)
            return (x - m) / jnp.sqrt(v + eps) * w + b

        def _block(x, state, ln1_w, ln1_b, ln2_w, ln2_b, maa_x, maa_w1, maa_w2, maa_stack, time_decay, td_w1, td_w2, u, Wr, Wk, Wv, Wg, Wo, gn_w, gn_b, ffn_maa_k, ffn_maa_r, Wfk, Wfr, Wfv):
            b, l, e = x.shape
            h = u.shape[0]
            s_ = e // h
            xa = _ln(x, ln1_w, ln1_b)
            sx = jnp.concatenate([state[:, 1:2] - xa[:, :1], xa[:, :-1] - xa[:, 1:]], axis=1)
            xxx = jnp.tanh((xa + sx * maa_x) @ maa_w1).reshape(b, l, 5, DM)
            xxx = jnp.einsum('blfd,fde->blfe', xxx, maa_w2)
            xm = xa[:, :, None] + sx[:, :, None] * (maa_stack + xxx)
            xk, xw, xv, xr, xg = (xm[:, :, j] for j in range(5))
            w = jnp.exp(-jnp.exp(time_decay + jnp.tanh(xw @ td_w1) @ td_w2)).reshape(b, l, h, s_)
            r = (xr @ Wr.T).reshape(b, l, h, s_)
            k = (xk @ Wk.T).reshape(b, l, h, s_)
            v = (xv @ Wv.T).reshape(b, l, h, s_)
            g = jax.nn.silu(xg @ Wg.T)
            s0 = state[:, 2:2 + s_].reshape(b, h, s_, s_)

            def step(s, rkvw):
                r_t, k_t, v_t, w_t = rkvw
                a = k_t[..., :, None] * v_t[..., None, :]
                out = jnp.einsum('bhi,bhij->bhj', r_t, u * a + s)
                s = a + w_t[..., :, None] * s
                return (s, out)
            rkvw = tuple((jnp.moveaxis(t, 1, 0) for t in (r, k, v, w)))
            _, out = jax.lax.scan(step, s0, rkvw)
            out = jnp.moveaxis(out, 0, 1).reshape(b, l, e)
            og = out.reshape(b, l, h, s_)
            m = og.mean(-1, keepdims=True)
            va = ((og - m) ** 2).mean(-1, keepdims=True)
            og = ((og - m) / jnp.sqrt(va + 1e-05)).reshape(b, l, e) * gn_w + gn_b
            x1 = x + og * g @ Wo.T
            xc = _ln(x1, ln2_w, ln2_b)
            sx2 = jnp.concatenate([state[:, 0:1] - xc[:, :1], xc[:, :-1] - xc[:, 1:]], axis=1)
            xk2 = xc + sx2 * ffn_maa_k
            xr2 = xc + sx2 * ffn_maa_r
            rr = jax.nn.sigmoid(xr2 @ Wfr.T)
            kk = jnp.square(jax.nn.relu(xk2 @ Wfk.T))
            return x1 + rr * (kk @ Wfv.T)
        return _block(x, state, ln1_w, ln1_b, ln2_w, ln2_b, maa_x, maa_w1, maa_w2, maa_stack, time_decay, td_w1, td_w2, u, Wr, Wk, Wv, Wg, Wo, gn_w, gn_b, ffn_maa_k, ffn_maa_r, Wfk, Wfr, Wfv)
    x = _L0_xattn_ref(x, ctx_2048, L0_xattn_ln1_w, L0_xattn_ln1_b, L0_xattn_ln2_w, L0_xattn_ln2_b, L0_xattn_maa_x, L0_xattn_maa_w1, L0_xattn_maa_w2, L0_xattn_maa_stack, L0_xattn_time_decay, L0_xattn_td_w1, L0_xattn_td_w2, L0_xattn_u, L0_xattn_Wr, L0_xattn_Wk, L0_xattn_Wv, L0_xattn_Wg, L0_xattn_Wo, L0_xattn_gn_w, L0_xattn_gn_b, L0_xattn_ffn_maa_k, L0_xattn_ffn_maa_r, L0_xattn_Wfk, L0_xattn_Wfr, L0_xattn_Wfv)
    return x

_drawn_inputs = setup_inputs


def setup_inputs(seed=0):
    import zlib

    import numpy as np

    out = dict(_drawn_inputs(seed))
    spreads = {'L0_xattn_ln1_w': (1.0, 0.554),
     'L0_xattn_ln1_b': (0.0, 0.565),
     'L0_xattn_ln2_w': (1.0, 0.6),
     'L0_xattn_ln2_b': (0.0, 0.8),
     'L0_xattn_gn_w': (1.0, 0.6),
     'L0_xattn_gn_b': (0.0, 0.8)}
    factors = {'ctx_2048': 8.0,
     'L0_xattn_maa_x': 8.0,
     'L0_xattn_maa_w1': 6.84,
     'L0_xattn_maa_w2': 6.756,
     'L0_xattn_time_decay': 2.719,
     'L0_xattn_td_w1': 8.0,
     'L0_xattn_td_w2': 8.0,
     'L0_xattn_u': 5.46,
     'L0_xattn_ffn_maa_k': 8.0,
     'L0_xattn_ffn_maa_r': 8.0,
     'L0_xattn_Wfk': 2.984,
     'L0_xattn_Wfr': 8.0,
     'L0_xattn_Wfv': 2.759}
    for name, (base, spread) in spreads.items():
        noise = np.random.default_rng([zlib.crc32(name.encode()), seed]).standard_normal(out[name].shape)
        drawn = base * np.exp(spread * noise) if base else spread * noise
        out[name] = jnp.asarray(drawn.astype(out[name].dtype))
    for name, factor in factors.items():
        out[name] = (out[name] * factor).astype(out[name].dtype)
    return out
```

```python
from contextlib import ExitStack

import numpy as np

import concourse.bass as bass
from concourse import mybir

ALU = mybir.AluOpType
ACT = mybir.ActivationFunctionType
F32 = mybir.dt.float32

B, L, E, H = 4, 256, 256, 32
S = E // H
P = 128
HALVES = E // P
TILES = L // P
G = P // H
Q = S // G
HH = P // S
DM, DD, NMIX = 32, 64, 5
MIX_W, MIX_K, MIX_V, MIX_R, MIX_G = 1, 0, 2, 3, 4
MIX_ORDER = (MIX_W, MIX_K, MIX_V, MIX_R, MIX_G)
CHUNKS = HALVES * G
EPS = 1e-5

VECS = ["ln1_w", "ln1_b", "ln2_w", "ln2_b", "maa_x", "maa0", "maa1", "maa2", "maa3", "maa4",
        "time_decay", "u", "ffn_maa_k", "ffn_maa_r", "gn_w", "gn_b"]
MATS = ["Wk", "Wv", "Wr", "Wg", "Wo", "Wfk", "Wfr", "Wfv"]


def constants():
    p, m = np.arange(P)[:, None], np.arange(P)[None, :]
    ident = (p == m)
    spread = [p == H * g + HH * half + m // S for half in range(HALVES) for g in range(G)]
    gather = [np.arange(H)[None, :] == HH * half + p // S for half in range(HALVES)]
    mean = (p % H == m % H) / S
    return np.concatenate([ident, *spread, *gather, mean], axis=1).astype(np.float32)


def rwkv_block(nc, x, state, vecs, consts, w1, w2, td1, td2, mats, out):
    with ExitStack() as ctx:
        def sb(name, shape, dt=F32):
            return ctx.enter_context(nc.sbuf_tensor(name, shape, dt))

        def bank(name):
            return ctx.enter_context(nc.psum_tensor(name, [P, HALVES * L], F32))

        def sem(name):
            return ctx.enter_context(nc.semaphore(name))

        vec_sb = sb("vec_sb", [P, len(VECS), HALVES])
        const_sb = sb("const_sb", [P, consts.shape[1]])
        ident = const_sb[:, 0:P]
        spread = const_sb[:, P:P + CHUNKS * P].rearrange("p (c m) -> p c m", m=P)
        gather = const_sb[:, P * (1 + CHUNKS):P * (1 + CHUNKS) + HALVES * H].rearrange("p (a h) -> p a h", h=H)
        head_mean = const_sb[:, P * (1 + CHUNKS) + HALVES * H:]
        bonus = sb("bonus", [P, HALVES, G, H])
        w1_sb = sb("w1_sb", [P, HALVES, NMIX * DM])
        w2_sb = sb("w2_sb", [P, NMIX, E])
        td1_sb = sb("td1_sb", [P, HALVES, DD])
        td2_sb = sb("td2_sb", [P, E])
        W = {m: sb(f"{m}_sb", [P, HALVES, E]) for m in MATS}
        state_rows = sb("state_rows", [B, 2, E])
        s0 = sb("s0", [P, HALVES, B, S])
        eps = sb("eps", [P, 1])

        x_sb = sb("x_sb", [P, B, TILES, E])
        xc = sb("xc", [P, B, HALVES, L + 1])
        k_sb = sb("k_sb", [P, B, HALVES, L])
        v_sb = sb("v_sb", [P, B, Q, L])
        g_sb = sb("g_sb", [P, B, Q, L])
        decay = sb("decay", [P, B, HALVES, Q, L])
        y_sb = sb("y_sb", [P, B, TILES, E])

        stats1 = sb("stats1", [P, B * TILES, 6])
        mv1 = sb("mv1", [P, B * TILES, 2])
        std1 = sb("std1", [P, B * TILES])
        rstd1 = sb("rstd1", [P, B * TILES])
        xn = sb("xn", [P, TILES, E])
        xa = sb("xa", [P, HALVES, L + 1])
        before = sb("before", [P, B, HALVES])
        r_sb = sb("r_sb", [P, HALVES, L])
        sx = sb("sx", [P, HALVES, L])
        xin = sb("xin", [P, HALVES, L])
        lora = sb("lora", [P, 2, L])
        td_hid = sb("td_hid", [P, L])
        xm = [sb(f"xm{j}", [P, HALVES, L]) for j in range(NMIX)]
        th_g = sb("th_g", [P, Q, L])
        ed = sb("ed", [P, HALVES, L])

        rec = sb("rec", [P, CHUNKS, Q, L])
        rk = sb("rk", [P, HALVES, L])
        vr = sb("vr", [P, Q, L])
        o_sb = sb("o_sb", [P, Q, L])
        cen = sb("cen", [P, Q, L])
        sq = sb("sq", [P, Q, L])
        std_o = sb("std_o", [P, L])
        rstd_o = sb("rstd_o", [P, L])
        on = sb("on", [P, Q, L])
        gated = sb("gated", [P, Q, L])

        x1 = sb("x1", [P, TILES, E])
        stats2 = sb("stats2", [P, TILES, 6])
        mdiff2, within2, msum2, between2, mean2, esq2 = (sb(n, [P, TILES]) for n in (
            "mdiff2", "within2", "msum2", "between2", "mean2", "esq2"))
        std2 = sb("std2", [P, TILES])
        rstd2 = sb("rstd2", [P, TILES])
        xn2 = sb("xn2", [P, TILES, E])
        sx2 = sb("sx2", [P, HALVES, L])
        xk2 = sb("xk2", [P, HALVES, L])
        xr2 = sb("xr2", [P, HALVES, L])
        relu = sb("relu", [P, HALVES, L])
        kk = sb("kk", [P, HALVES, L])
        th_r = sb("th_r", [P, TILES, E])
        f1 = sb("f1", [P, TILES, E])

        pa = [bank(f"pa{i}") for i in range(3)]
        pv = [bank(f"pv{i}") for i in range(2)]
        py = bank("py")
        pc = [bank(f"pc{i}") for i in range(2)]

        def by2(b):
            return b[:].rearrange("p (a t) -> p a t", a=2)

        def vcol(name, a):
            return vec_sb[:, VECS.index(name), a:a + 1]

        x_in, vec_in, const_in, state_in, w_in = (sem(n) for n in ("x_in", "vec_in", "const_in", "state_in", "w_in"))
        w1_in, w2_in, td_in, out_done = (sem(n) for n in ("w1_in", "w2_in", "td_in", "out_done"))
        mat_in = {m: sem(f"{m}_in") for m in MATS}
        zeroed, stats1_ready, mv1_ready, std1_ready, rstd1_ready = (sem(n) for n in (
            "zeroed", "stats1_ready", "mv1_ready", "std1_ready", "rstd1_ready"))
        state_tr_done, state_cols_ready, bonus_ready = (sem(n) for n in ("state_tr_done", "state_cols_ready", "bonus_ready"))
        xn_ready, sx_ready, xin_ready, m_ready, g_ready = (sem(n) for n in (
            "xn_ready", "sx_ready", "xin_ready", "m_ready", "g_ready"))
        a_ready, scan_done, vr_ready, o_ready, cen_ready, rstdo_ready = (sem(n) for n in (
            "a_ready", "scan_done", "vr_ready", "o_ready", "cen_ready", "rstdo_ready"))
        on_ready, gated_ready, x1_ready, stats2_ready, mv2_ready, rstd2_ready = (sem(n) for n in (
            "on_ready", "gated_ready", "x1_ready", "stats2_ready", "mv2_ready", "rstd2_ready"))
        xn2_ready, xk2_ready, xr2_ready, f1_ready, y_ready = (sem(n) for n in (
            "xn2_ready", "xk2_ready", "xr2_ready", "f1_ready", "y_ready"))
        mdiff_ready, between_ready = sem("mdiff_ready"), sem("between_ready")
        xa_ready, lora_ready, tdh_ready, k_ready, v_ready, r_ready, thg_ready, ed_ready, w_ready = (sem(n) for n in (
            "xa_ready", "lora_ready", "tdh_ready", "k_ready", "v_ready", "r_ready", "thg_ready", "ed_ready",
            "w_ready"))
        sq_ready, stdo_ready, std2_ready, xc_ready, relu_ready, kk_ready, thr_ready = (sem(n) for n in (
            "sq_ready", "stdo_ready", "std2_ready", "xc_ready", "relu_ready", "kk_ready", "thr_ready"))
        xm_ready, s0_placed, p_ready, rk_ready, sx2_ready = (sem(n) for n in (
            "xm_ready", "s0_placed", "p_ready", "rk_ready", "sx2_ready"))
        tr1_done, w1_done, w2_done, td1_done, td2_done, pk_done, pvv_done, pr_done, pg_done = (sem(n) for n in (
            "tr1_done", "w1_done", "w2_done", "td1_done", "td2_done", "pk_done", "pvv_done", "pr_done",
            "pg_done"))
        spread_done, gather_done, bonus_done, mean_done, var_done = (sem(n) for n in (
            "spread_done", "gather_done", "bonus_done", "mean_done", "var_done"))
        wo_done, tr2_done, fk_done, fr_done, fv_done = (sem(n) for n in (
            "wo_done", "tr2_done", "fk_done", "fr_done", "fv_done"))

        block = ctx.enter_context(nc.Block())

        @block.sync
        def _(sp):
            sp.dma_start(x_sb[:], x.rearrange("b (t p) e -> p b t e", p=P)).then_inc(x_in, 16)
            sp.dma_start(vec_sb[:], vecs).then_inc(vec_in, 16)
            sp.dma_start(state_rows[:], state[:, 0:2, :]).then_inc(state_in, 16)
            sp.dma_start(const_sb[:], consts).then_inc(const_in, 16)
            sp.wait_ge(zeroed, 2)
            for j in range(NMIX):
                row = DM * (j % G)
                sp.dma_start(w2_sb[row:row + DM, j, :], w2[j]).then_inc(w2_in, 16)
            sp.dma_start(td1_sb[:], td1.rearrange("(a p) n -> p a n", p=P)).then_inc(td_in, 16)
            sp.dma_start(td2_sb[0:DD, :], td2).then_inc(td_in, 16)
            for m in ("Wv", "Wg", "Wfk", "Wfv"):
                sp.dma_start(W[m][:], mats[m].rearrange("(a p) n -> p a n", p=P)).then_inc(mat_in[m], 16)
            with sp.Fori(0, B) as b:
                sp.wait_ge(y_ready, b + 1)
                sp.dma_start(out[b].rearrange("(t p) e -> p t e", p=P), y_sb[:, b]).then_inc(out_done, 16)
            sp.wait_ge(out_done, 16 * B)

        @block.gpsimd
        def _(pool):
            def s0_place(b):
                for a in range(HALVES):
                    dst = rec[:, G * a:G * a + G, :, 0]
                    src = s0[:, a, b, :].rearrange("p (q g) -> p g q", g=G)
                    nc.gpsimd.tensor_copy(dst, src).then_inc(s0_placed, 1)

            def product(b, c):
                if c == 0:
                    pool.wait_ge(r_ready, b + 1)
                pool.wait_ge(scan_done, CHUNKS * b + c + 1)
                r_b = r_sb[:, c // G, :].unsqueeze(1).broadcast_to([P, Q, L])
                nc.gpsimd.tensor_tensor(rec[:, c], rec[:, c], r_b, ALU.mult).then_inc(p_ready, 1)

            def mixed(n, i):
                j = MIX_ORDER[i]
                pool.wait_ge(m_ready, 10 * n + 2 * i + 2)
                nc.gpsimd.tensor_tensor(xm[j][:], xm[j][:], xa[:, :, 1:L + 1], ALU.add).then_inc(xm_ready, 1)

            def rk_product(b):
                pool.wait_ge(k_ready, b + 1)
                nc.gpsimd.tensor_tensor(rk[:], r_sb[:], k_sb[:, b], ALU.mult).then_inc(rk_ready, 1)

            def shift2(b):
                pool.wait_ge(xc_ready, 2 * b + 2)
                nc.gpsimd.tensor_tensor(sx2[:], xc[:, b, :, 0:L], xc[:, b, :, 1:L + 1],
                                        ALU.subtract).then_inc(sx2_ready, 1)

            def round_(n, b):
                if b is not None:
                    s0_place(b)
                    for c in range(4):
                        product(b, c)
                if n is not None:
                    mixed(n, 0)
                    mixed(n, 1)
                if b is not None:
                    product(b, 4)
                if n is not None:
                    mixed(n, 2)
                if b is not None:
                    product(b, 5)
                    rk_product(b)
                    product(b, 6)
                    product(b, 7)
                if n is not None:
                    mixed(n, 3)
                    mixed(n, 4)
                if b is not None:
                    shift2(b)

            nc.gpsimd.memset(w2_sb[:], 0.0).then_inc(zeroed, 1)
            nc.gpsimd.memset(td2_sb[:], 0.0).then_inc(zeroed, 1)
            nc.gpsimd.memset(lora[:], 0.0).then_inc(zeroed, 1)
            nc.gpsimd.memset(td_hid[:], 0.0).then_inc(zeroed, 1)
            nc.gpsimd.memset(decay[:, :, :, :, 0], 0.0).then_inc(zeroed, 1)
            nc.gpsimd.memset(eps[:], EPS).then_inc(zeroed, 1)
            pool.wait_ge(state_in, 48)
            round_(0, None)
            with pool.Fori(0, B - 1) as b:
                round_(b + 1, b)
            round_(None, B - 1)

        @block.scalar
        def _(act):
            act.dma_start(w1_sb[:], w1.rearrange("(a p) n -> p a n", p=P)).then_inc(w1_in, 16)
            for m in ("Wk", "Wr", "Wo", "Wfr"):
                act.dma_start(W[m][:], mats[m].rearrange("(a p) n -> p a n", p=P)).then_inc(mat_in[m], 16)
            s0_rows = state.rearrange("b r e -> b (r e)")[:, 2 * E:(2 + S) * E]
            for a in range(HALVES):
                half = s0_rows[:, a * P * S:(a + 1) * P * S]
                act.dma_start(s0[:, a], half.rearrange("b (p j) -> p b j", j=S)).then_inc(state_in, 16)

            def norm1(n):
                act.wait_ge(tr1_done, n + 1)
                if not isinstance(n, int) or n:
                    act.wait_ge(xm_ready, NMIX * n)
                nc.scalar.activation(xa[:, :, 0], before[:, n, :], ACT.Copy).then_inc(xa_ready, 1)
                for a in range(HALVES):
                    nc.scalar.activation(xa[:, a, 1:L + 1], pa[0][:, a * L:(a + 1) * L], ACT.Identity,
                                         bias=vcol("ln1_b", a), scale=vcol("ln1_w", a)).then_inc(xa_ready, 1)

            def lora_tanh(n):
                act.wait_ge(w1_done, n + 1)
                if not isinstance(n, int) or n:
                    act.wait_ge(w2_done, 5 * n)
                nc.scalar.activation(lora[:, 0, :], pa[1][:, 0:L], ACT.Tanh).then_inc(lora_ready, 1)
                nc.scalar.activation(lora[0:DM, 1, :], pa[1][0:DM, L:2 * L], ACT.Tanh).then_inc(lora_ready, 1)

            def td_tanh(n):
                act.wait_ge(td1_done, n + 1)
                nc.scalar.activation(td_hid[0:DD, :], pa[2][0:DD, 0:L], ACT.Tanh).then_inc(tdh_ready, 1)

            def take(n, done, ready, dst, src):
                act.wait_ge(done, n + 1)
                nc.scalar.activation(dst[:, n], by2(src), ACT.Copy).then_inc(ready, 1)

            def take_r(n):
                act.wait_ge(pr_done, n + 1)
                if not isinstance(n, int) or n:
                    act.wait_ge(p_ready, CHUNKS * n)
                nc.scalar.activation(r_sb[:], by2(pa[2]), ACT.Copy).then_inc(r_ready, 1)

            def decays(n):
                act.wait_ge(td2_done, n + 1)
                if not isinstance(n, int) or n:
                    act.wait_ge(w_ready, 2 * n)
                for a in range(HALVES):
                    nc.scalar.activation(ed[:, a, :], pa[2][:, a * L:(a + 1) * L], ACT.Exp,
                                         bias=vcol("time_decay", a)).then_inc(ed_ready, 1)
                act.wait_ge(ed_ready, 2 * n + 2)
                for q in range(Q):
                    nc.scalar.activation(decay[:, n, :, q, 1:L], ed[:, :, 0:L - 1], ACT.Exp,
                                         scale=-1.0).then_inc(w_ready, 1)

            def gate_tanh(n):
                act.wait_ge(pg_done, n + 1)
                nc.scalar.activation(th_g[:], by2(pa[0]), ACT.Tanh, scale=0.5).then_inc(thg_ready, 1)

            def squares(b):
                act.wait_ge(cen_ready, b + 1)
                nc.scalar.activation(sq[:], cen[:], ACT.Square).then_inc(sq_ready, 1)

            def head_std(b):
                act.wait_ge(var_done, b + 1)
                nc.scalar.activation(std_o[:], pc[0][:, 0:L], ACT.Sqrt, bias=eps[:]).then_inc(stdo_ready, 1)

            def token_std(b):
                act.wait_ge(mv2_ready, b + 1)
                nc.scalar.activation(std2[:], esq2[:], ACT.Sqrt, bias=eps[:], scale=1.0 / E).then_inc(std2_ready, 1)

            def norm2(b):
                act.wait_ge(tr2_done, b + 1)
                for a in range(HALVES):
                    nc.scalar.activation(xc[:, b, a, 1:L + 1], pc[0][:, a * L:(a + 1) * L], ACT.Identity,
                                         bias=vcol("ln2_b", a), scale=vcol("ln2_w", a)).then_inc(xc_ready, 1)

            def relu_squared(b):
                act.wait_ge(fk_done, b + 1)
                nc.scalar.activation(relu[:], by2(pc[1]), ACT.Relu).then_inc(relu_ready, 1)
                act.wait_ge(relu_ready, b + 1)
                nc.scalar.activation(kk[:], relu[:], ACT.Square).then_inc(kk_ready, 1)

            def receptance_tanh(b):
                act.wait_ge(fr_done, b + 1)
                nc.scalar.activation(th_r[:], by2(pc[0]), ACT.Tanh, scale=0.5).then_inc(thr_ready, 1)

            def round_(n, b):
                if n is not None:
                    norm1(n)
                    lora_tanh(n)
                    td_tanh(n)
                    take(n, pk_done, k_ready, k_sb, pa[1])
                    decays(n)
                if b is not None:
                    squares(b)
                if n is not None:
                    take(n, pvv_done, v_ready, v_sb, pa[1])
                if b is not None:
                    head_std(b)
                if n is not None:
                    take_r(n)
                if b is not None:
                    token_std(b)
                if n is not None:
                    gate_tanh(n)
                if b is not None:
                    norm2(b)
                    relu_squared(b)
                    receptance_tanh(b)

            act.wait_ge(mv1_ready, B * TILES)
            act.wait_ge(zeroed, 6)
            nc.scalar.activation(std1[:], mv1[:, :, 1], ACT.Sqrt, bias=eps[:]).then_inc(std1_ready, 1)
            act.wait_ge(state_tr_done, 1)
            rows = pc[0][:, 0:2 * 2 * B].rearrange("p (a r b) -> p b a r", a=HALVES, r=2)
            nc.scalar.activation(before[:], rows[:, :, :, 1], ACT.Copy).then_inc(state_cols_ready, 1)
            nc.scalar.activation(xc[:, :, :, 0], rows[:, :, :, 0], ACT.Copy).then_inc(state_cols_ready, 1)
            act.wait_ge(vec_in, 16)
            round_(0, None)
            with act.Fori(0, B - 1) as b:
                round_(b + 1, b)
            round_(None, B - 1)

        @block.vector
        def _(dve):
            def normalise1(n):
                if not isinstance(n, int) or n:
                    dve.wait_ge(tr1_done, n)
                for t in range(TILES):
                    i = n * TILES + t
                    nc.vector.tensor_scalar(xn[:, t, :], x_sb[:, n, t, :], mv1[:, bass.ds(i, 1), 0],
                                            rstd1[:, bass.ds(i, 1)], ALU.subtract, ALU.mult).then_inc(xn_ready, 1)

            def shift1(n):
                dve.wait_ge(xa_ready, 3 * n + 3)
                nc.vector.tensor_tensor(sx[:], xa[:, :, 0:L], xa[:, :, 1:L + 1],
                                        ALU.subtract).then_inc(sx_ready, 1)
                dve.wait_ge(sx_ready, n + 1)
                for a in range(HALVES):
                    nc.vector.scalar_tensor_tensor(xin[:, a, :], sx[:, a, :], vcol("maa_x", a), xa[:, a, 1:L + 1],
                                                   ALU.mult, ALU.add).then_inc(xin_ready, 1)

            def mix(n, i):
                j = MIX_ORDER[i]
                src = pa[(2, 0, 1, 0, 0)[i]]
                dve.wait_ge(w2_done, 5 * n + i + 1)
                for a in range(HALVES):
                    nc.vector.scalar_tensor_tensor(xm[j][:, a, :], src[:, a * L:(a + 1) * L], vcol(f"maa{j}", a),
                                                   sx[:, a, :], ALU.add, ALU.mult).then_inc(m_ready, 1)

            def gate(n):
                dve.wait_ge(thg_ready, n + 1)
                nc.vector.scalar_tensor_tensor(g_sb[:, n], th_g[:], 1.0, by2(pa[0]), ALU.add,
                                               ALU.mult).then_inc(g_ready, 1)

            def kv(b, c):
                if c == 0:
                    dve.wait_ge(k_ready, b + 1)
                    dve.wait_ge(s0_placed, 2 * b + 2)
                dve.wait_ge(spread_done, CHUNKS * b + c + 1)
                k_b = k_sb[:, b, c // G, 0:L - 1].unsqueeze(1).broadcast_to([P, Q, L - 1])
                nc.vector.tensor_tensor(rec[:, c, :, 1:L], by2(pv[c % 2])[:, :, 0:L - 1], k_b,
                                        ALU.mult).then_inc(a_ready, 1)

            def scan(b, c):
                if c == 0:
                    dve.wait_ge(w_ready, 2 * b + 2)
                dve.wait_ge(a_ready, CHUNKS * b + c + 1)
                rows = rec[:, c].rearrange("p q t -> p (q t)")
                nc.vector.tensor_tensor_scan(rows, decay[:, b, c // G].rearrange("p q t -> p (q t)"), rows, 0.0,
                                             ALU.mult, ALU.add).then_inc(scan_done, 1)

            def wkv_out(b):
                dve.wait_ge(bonus_done, b + 1)
                rb = pc[0][:, 0:L].unsqueeze(1).broadcast_to([P, Q, L])
                nc.vector.tensor_tensor(vr[:], rb, v_sb[:, b], ALU.mult).then_inc(vr_ready, 1)
                dve.wait_ge(vr_ready, b + 1)
                nc.vector.tensor_tensor(o_sb[:], by2(py), vr[:], ALU.add).then_inc(o_ready, 1)

            def centre(b):
                dve.wait_ge(mean_done, b + 1)
                mean = pc[1][:, 0:L].unsqueeze(1).broadcast_to([P, Q, L])
                nc.vector.tensor_tensor(cen[:], o_sb[:], mean, ALU.subtract).then_inc(cen_ready, 1)

            def gated_norm(b):
                dve.wait_ge(stdo_ready, b + 1)
                nc.vector.reciprocal(rstd_o[:], std_o[:]).then_inc(rstdo_ready, 1)
                dve.wait_ge(rstdo_ready, b + 1)
                for q in range(Q):
                    nc.vector.scalar_tensor_tensor(on[:, q, :], cen[:, q, :], vcol("gn_w", q), rstd_o[:], ALU.mult,
                                                   ALU.mult).then_inc(on_ready, 1)
                for q in range(Q):
                    dve.wait_ge(on_ready, 2 * b + q + 1)
                    nc.vector.scalar_tensor_tensor(gated[:, q, :], on[:, q, :], vcol("gn_b", q), g_sb[:, b, q, :],
                                                   ALU.add, ALU.mult).then_inc(gated_ready, 1)

            def residual(b):
                dve.wait_ge(wo_done, b + 1)
                nc.vector.scalar_tensor_tensor(x1[:], by2(pc[1]), 0.5, x_sb[:, b], ALU.mult,
                                               ALU.add).then_inc(x1_ready, 1)
                dve.wait_ge(x1_ready, b + 1)
                for t in range(TILES):
                    nc.vector.bn_stats(stats2[:, t, :], x1[:, t, :]).then_inc(stats2_ready, 1)
                dve.wait_ge(stats2_ready, 2 * b + 2)
                nc.vector.tensor_tensor(mdiff2[:], stats2[:, :, 1], stats2[:, :, 4], ALU.subtract).then_inc(mdiff_ready, 1)
                nc.vector.tensor_tensor(within2[:], stats2[:, :, 2], stats2[:, :, 5], ALU.add).then_inc(mdiff_ready, 1)
                nc.vector.tensor_tensor(msum2[:], stats2[:, :, 1], stats2[:, :, 4], ALU.add).then_inc(mdiff_ready, 1)
                dve.wait_ge(mdiff_ready, 3 * b + 3)
                nc.vector.tensor_tensor(between2[:], mdiff2[:], mdiff2[:], ALU.mult).then_inc(between_ready, 1)
                nc.vector.tensor_scalar(mean2[:], msum2[:], 0.5, None, ALU.mult).then_inc(between_ready, 1)
                dve.wait_ge(between_ready, 2 * b + 2)
                nc.vector.scalar_tensor_tensor(esq2[:], between2[:], E / 4, within2[:], ALU.mult,
                                               ALU.add).then_inc(mv2_ready, 1)
                dve.wait_ge(std2_ready, b + 1)
                nc.vector.reciprocal(rstd2[:], std2[:]).then_inc(rstd2_ready, 1)
                dve.wait_ge(rstd2_ready, b + 1)
                for t in range(TILES):
                    nc.vector.tensor_scalar(xn2[:, t, :], x1[:, t, :], mean2[:, t:t + 1], rstd2[:, t:t + 1],
                                            ALU.subtract, ALU.mult).then_inc(xn2_ready, 1)

            def mix2(b):
                dve.wait_ge(sx2_ready, b + 1)
                for name, dst, ready in (("ffn_maa_k", xk2, xk2_ready), ("ffn_maa_r", xr2, xr2_ready)):
                    for a in range(HALVES):
                        nc.vector.scalar_tensor_tensor(dst[:, a, :], sx2[:, a, :], vcol(name, a),
                                                       xc[:, b, a, 1:L + 1], ALU.mult, ALU.add).then_inc(ready, 1)

            def finish(b):
                dve.wait_ge(thr_ready, b + 1)
                dve.wait_ge(fv_done, b + 1)
                nc.vector.scalar_tensor_tensor(f1[:], th_r[:], 1.0, by2(pc[1]), ALU.add, ALU.mult).then_inc(f1_ready, 1)
                dve.wait_ge(f1_ready, b + 1)
                nc.vector.scalar_tensor_tensor(y_sb[:, b], f1[:], 0.5, x1[:], ALU.mult, ALU.add).then_inc(y_ready, 1)

            def round_(n, b):
                if b is not None:
                    kv(b, 0)
                    kv(b, 1)
                    scan(b, 0)
                if n is not None:
                    normalise1(n)
                if b is not None:
                    scan(b, 1)
                    kv(b, 2)
                    kv(b, 3)
                    scan(b, 2)
                if n is not None:
                    shift1(n)
                if b is not None:
                    scan(b, 3)
                    kv(b, 4)
                    kv(b, 5)
                    scan(b, 4)
                if n is not None:
                    mix(n, 0)
                    mix(n, 1)
                if b is not None:
                    scan(b, 5)
                    kv(b, 6)
                    kv(b, 7)
                    scan(b, 6)
                if n is not None:
                    mix(n, 2)
                if b is not None:
                    scan(b, 7)
                if n is not None:
                    mix(n, 3)
                if b is not None:
                    wkv_out(b)
                if n is not None:
                    mix(n, 4)
                if b is not None:
                    centre(b)
                    gated_norm(b)
                    residual(b)
                if n is not None:
                    gate(n)
                if b is not None:
                    mix2(b)
                    finish(b)

            dve.wait_ge(x_in, 16)
            for i in range(B * TILES):
                nc.vector.bn_stats(stats1[:, i, :], x_sb[:, i // TILES, i % TILES, :]).then_inc(stats1_ready, 1)
            for i in range(B * TILES):
                dve.wait_ge(stats1_ready, i + 1)
                nc.vector.bn_aggr(mv1[:, i, :], stats1[:, i, :]).then_inc(mv1_ready, 1)
            dve.wait_ge(std1_ready, 1)
            nc.vector.reciprocal(rstd1[:], std1[:]).then_inc(rstd1_ready, 1)
            dve.wait_ge(rstd1_ready, 1)
            dve.wait_ge(vec_in, 16)
            dve.wait_ge(const_in, 16)
            for a in range(HALVES):
                g_b = gather[:, a, :].unsqueeze(1).broadcast_to([P, G, H])
                nc.vector.tensor_scalar(bonus[:, a], g_b, vcol("u", a), None, ALU.mult).then_inc(bonus_ready, 1)
            dve.wait_ge(state_cols_ready, 2)
            round_(0, None)
            with dve.Fori(0, B - 1) as b:
                round_(b + 1, b)
            round_(None, B - 1)

        @block.tensor
        def _(pe):
            def two_halves(dst, w, rhs, m=P, cols=HALVES):
                for o in range(cols):
                    for a in range(HALVES):
                        mm = nc.tensor.matmul(dst[0:m, o * L:(o + 1) * L], w[:, a, o * m:(o + 1) * m], rhs[:, a, :],
                                              start=(a == 0), stop=(a == HALVES - 1))
                return mm

            def token_major(dst, act_t, w):
                for t in range(TILES):
                    for a in range(HALVES):
                        mm = nc.tensor.matmul(dst[:, t * E:(t + 1) * E], act_t[:, a, t * P:(t + 1) * P], w[:, a, :],
                                              start=(a == 0), stop=(a == HALVES - 1))
                return mm

            def transposes(dst, src, done):
                for a in range(HALVES):
                    for t in range(TILES):
                        mm = nc.tensor.transpose(dst[:, a * L + t * P:a * L + (t + 1) * P],
                                                 src[:, t, a * P:(a + 1) * P], ident)
                mm.then_inc(done, 1)

            def tr1(n):
                pe.wait_ge(xn_ready, 2 * n + 2)
                if not isinstance(n, int) or n:
                    pe.wait_ge(g_ready, n)
                transposes(pa[0], xn, tr1_done)

            def lora_in(n):
                pe.wait_ge(xin_ready, 2 * n + 2)
                if not isinstance(n, int) or n:
                    pe.wait_ge(v_ready, n)
                for a in range(HALVES):
                    nc.tensor.matmul(pa[1][:, 0:L], w1_sb[:, a, 0:P], xin[:, a, :], start=(a == 0),
                                     stop=(a == HALVES - 1))
                for a in range(HALVES):
                    mm = nc.tensor.matmul(pa[1][0:DM, L:2 * L], w1_sb[:, a, P:P + DM], xin[:, a, :],
                                          start=(a == 0), stop=(a == HALVES - 1))
                mm.then_inc(w1_done, 1)

            def lora_out(n, i):
                j = MIX_ORDER[i]
                if i == 0:
                    pe.wait_ge(lora_ready, 2 * n + 2)
                    if not isinstance(n, int) or n:
                        pe.wait_ge(r_ready, n)
                elif i == 1:
                    pe.wait_ge(xa_ready, 3 * n + 3)
                elif i == 3:
                    pe.wait_ge(m_ready, 10 * n + 4)
                elif i == 4:
                    pe.wait_ge(m_ready, 10 * n + 8)
                dst = pa[(2, 0, 1, 0, 0)[i]]
                for o in range(HALVES):
                    mm = nc.tensor.matmul(dst[:, o * L:(o + 1) * L], w2_sb[:, j, o * P:(o + 1) * P],
                                          lora[:, j // G, :], start=True, stop=True)
                mm.then_inc(w2_done, 1)

            def td_in_(n):
                pe.wait_ge(xm_ready, 5 * n + 1)
                two_halves(pa[2], td1_sb, xm[MIX_W], m=DD, cols=1).then_inc(td1_done, 1)

            def td_out(n):
                pe.wait_ge(tdh_ready, n + 1)
                for o in range(HALVES):
                    mm = nc.tensor.matmul(pa[2][:, o * L:(o + 1) * L], td2_sb[:, o * P:(o + 1) * P], td_hid[:],
                                          start=True, stop=True)
                mm.then_inc(td2_done, 1)

            def project_k(n):
                pe.wait_ge(m_ready, 10 * n + 6)
                pe.wait_ge(xm_ready, 5 * n + 2)
                two_halves(pa[1], W["Wk"], xm[MIX_K]).then_inc(pk_done, 1)

            def project_v(n):
                pe.wait_ge(k_ready, n + 1)
                pe.wait_ge(xm_ready, 5 * n + 3)
                two_halves(pa[1], W["Wv"], xm[MIX_V]).then_inc(pvv_done, 1)

            def project_r(n):
                pe.wait_ge(ed_ready, 2 * n + 2)
                pe.wait_ge(xm_ready, 5 * n + 4)
                two_halves(pa[2], W["Wr"], xm[MIX_R]).then_inc(pr_done, 1)

            def project_g(n):
                pe.wait_ge(xm_ready, 5 * n + 5)
                two_halves(pa[0], W["Wg"], xm[MIX_G]).then_inc(pg_done, 1)

            def spread_v(b, c):
                if c == 0:
                    pe.wait_ge(v_ready, b + 1)
                if c >= 2:
                    pe.wait_ge(a_ready, CHUNKS * b + c - 1)
                nc.tensor.matmul(pv[c % 2][:], spread[:, c, :], v_sb[:, b].rearrange("p q t -> p (q t)"), start=True,
                                 stop=True).then_inc(spread_done, 1)

            def gather_half(b, a):
                pe.wait_ge(p_ready, CHUNKS * b + G * (a + 1))
                for g in range(G):
                    mm = nc.tensor.matmul(py[H * g:H * (g + 1), :], gather[:, a, :],
                                          rec[:, G * a + g].rearrange("p q t -> p (q t)"), start=(a == 0),
                                          stop=(a == HALVES - 1))
                mm.then_inc(gather_done, 1)

            def bonus_sum(b):
                pe.wait_ge(rk_ready, b + 1)
                if isinstance(b, int):
                    pe.wait_ge(thr_ready, b)
                for a in range(HALVES):
                    mm = nc.tensor.matmul(pc[0][:, 0:L], bonus[:, a].rearrange("p g h -> p (g h)"), rk[:, a, :],
                                          start=(a == 0), stop=(a == HALVES - 1))
                mm.then_inc(bonus_done, 1)

            def head_sum(dst, src, done):
                for q in range(Q):
                    mm = nc.tensor.matmul(dst[:, 0:L], head_mean, src[:, q, :], start=(q == 0), stop=(q == Q - 1))
                mm.then_inc(done, 1)

            def mean_(b):
                pe.wait_ge(o_ready, b + 1)
                if isinstance(b, int):
                    pe.wait_ge(f1_ready, b)
                head_sum(pc[1], o_sb, mean_done)

            def var_(b):
                pe.wait_ge(sq_ready, b + 1)
                head_sum(pc[0], sq, var_done)

            def out_product(b):
                pe.wait_ge(gated_ready, 2 * b + 2)
                token_major(pc[1], gated, W["Wo"]).then_inc(wo_done, 1)

            def tr2(b):
                pe.wait_ge(xn2_ready, 2 * b + 2)
                transposes(pc[0], xn2, tr2_done)

            def ffn_k(b):
                pe.wait_ge(xk2_ready, 2 * b + 2)
                two_halves(pc[1], W["Wfk"], xk2).then_inc(fk_done, 1)

            def ffn_r(b):
                pe.wait_ge(xr2_ready, 2 * b + 2)
                token_major(pc[0], xr2, W["Wfr"]).then_inc(fr_done, 1)

            def ffn_v(b):
                pe.wait_ge(kk_ready, b + 1)
                token_major(pc[1], kk, W["Wfv"]).then_inc(fv_done, 1)

            def round_(n, b, first=False):
                if b is not None:
                    spread_v(b, 0)
                    spread_v(b, 1)
                if n is not None:
                    tr1(n)
                if b is not None:
                    spread_v(b, 2)
                    spread_v(b, 3)
                if n is not None:
                    if first:
                        pe.wait_ge(w1_in, 16)
                    lora_in(n)
                if b is not None:
                    spread_v(b, 4)
                    spread_v(b, 5)
                if n is not None:
                    if first:
                        pe.wait_ge(w2_in, 16 * NMIX)
                        pe.wait_ge(td_in, 32)
                        pe.wait_ge(zeroed, 6)
                    lora_out(n, 0)
                    lora_out(n, 1)
                if b is not None:
                    spread_v(b, 6)
                    spread_v(b, 7)
                if n is not None:
                    lora_out(n, 2)
                    td_in_(n)
                    lora_out(n, 3)
                if b is not None:
                    gather_half(b, 0)
                if n is not None:
                    if first:
                        for m in MATS:
                            pe.wait_ge(mat_in[m], 16)
                    project_k(n)
                    td_out(n)
                if b is not None:
                    gather_half(b, 1)
                    bonus_sum(b)
                if n is not None:
                    lora_out(n, 4)
                if b is not None:
                    mean_(b)
                if n is not None:
                    project_v(n)
                if b is not None:
                    var_(b)
                if n is not None:
                    project_r(n)
                if b is not None:
                    out_product(b)
                if n is not None:
                    project_g(n)
                if b is not None:
                    tr2(b)
                    ffn_k(b)
                    ffn_r(b)
                    ffn_v(b)

            pe.wait_ge(const_in, 16)
            pe.wait_ge(state_in, 48)
            pe.wait_ge(bonus_ready, 2)
            for a in range(HALVES):
                for r in range(2):
                    col = (a * 2 + r) * B
                    mm = nc.tensor.transpose(pc[0][:, col:col + B], state_rows[:, r, a * P:(a + 1) * P],
                                             ident[0:B, 0:B])
            mm.then_inc(state_tr_done, 1)
            round_(0, None, first=True)
            with pe.Fori(0, B - 1) as b:
                round_(b + 1, b)
            round_(None, B - 1)


PRE = "L0_xattn_"


def kernel(**inputs):
    import concourse.bacc as _bacc
    from concourse.bass_utils import run_bass_kernel_spmd as _run

    def get(name):
        return np.asarray(inputs[PRE + name])

    def halves(v):
        return v.reshape(HALVES, P).T

    def grouped(v):
        return v.reshape(H, Q, G).transpose(2, 0, 1).reshape(P, Q)

    def grouped_out(m):
        return m.reshape(H, Q, G, E).transpose(3, 1, 2, 0).reshape(E, E)

    maa = get("maa_stack").reshape(NMIX, E)
    cols = []
    for name in VECS:
        if name.startswith("gn_"):
            cols.append(grouped(get(name)))
        elif name[:3] == "maa" and name[3:].isdigit():
            cols.append(halves(maa[int(name[3:])]))
        else:
            cols.append(halves(get(name).reshape(E)))
    arrays = {
        "x": np.asarray(inputs["x"]),
        "state": np.asarray(inputs["ctx_2048"]),
        "vecs": np.stack(cols, axis=1),
        "consts": constants(),
        "w1": get("maa_w1"),
        "w2": get("maa_w2"),
        "td1": get("td_w1"),
        "td2": get("td_w2"),
        "Wk": get("Wk").T,
        "Wr": get("Wr").T,
        "Wv": grouped_out(get("Wv")),
        "Wg": grouped_out(get("Wg")),
        "Wo": get("Wo").reshape(E, H, Q, G).transpose(2, 3, 1, 0).reshape(E, E),
        "Wfk": get("Wfk").T,
        "Wfr": get("Wfr").T,
        "Wfv": get("Wfv").T,
    }
    arrays = {f"in_{n}": np.ascontiguousarray(a) for n, a in arrays.items()}
    nc = _bacc.Bacc("TRN2", target_bir_lowering=False, num_devices=1)
    d = {n[3:]: nc.dram_tensor(n, a.shape, mybir.dt.from_np(a.dtype), kind="ExternalInput").ap()
         for n, a in arrays.items()}
    out = nc.dram_tensor("out_0", (B, L, E), F32, kind="ExternalOutput").ap()
    rwkv_block(nc, d["x"], d["state"], d["vecs"], d["consts"], d["w1"], d["w2"], d["td1"], d["td2"],
               {m: d[m] for m in MATS}, out)
    r = _run(nc, [arrays], core_ids=[0])
    return r.results[0]["out_0"]
```

```python
from contextlib import ExitStack

import numpy as np

import concourse.bass as bass
from concourse import mybir

ALU = mybir.AluOpType
ACT = mybir.ActivationFunctionType
F32 = mybir.dt.float32
F32R = mybir.dt.float32r

B, L, E, H = 4, 256, 256, 32
S = E // H
P = 128
HALVES = E // P
TILES = L // P
G = P // H
Q = S // G
HH = P // S
DM, DD, NMIX = 32, 64, 5
MIX_W, MIX_K, MIX_V, MIX_R, MIX_G = 1, 0, 2, 3, 4
MIX_ORDER = (MIX_K, MIX_V, MIX_W, MIX_R, MIX_G)
CHUNKS = HALVES * G
TB = L // G
EPS = 1e-5

VECS = ["ln1_w", "ln1_b", "ln2_w", "ln2_b", "maa_x", "maa0", "maa1", "maa2", "maa3", "maa4",
        "time_decay", "u", "ffn_maa_k", "ffn_maa_r", "gn_w", "gn_b"]
MATS = ["Wk", "Wv", "Wr", "Wg", "Wo", "Wfk", "Wfr", "Wfv"]


def constants():
    p, m = np.arange(P)[:, None], np.arange(P)[None, :]
    ident = (p == m)
    spread = [p == H * g + HH * half + m // S for half in range(HALVES) for g in range(G)]
    gather = [np.arange(H)[None, :] == HH * half + p // S for half in range(HALVES)]
    mean = (p % H == m % H) / S
    unblock = [p == H * tb + m % H for tb in range(G)]
    return np.concatenate([ident, *spread, *gather, mean, mean[:, 0:H], *unblock], axis=1).astype(np.float32)


def rwkv_block(nc, x, state, vecs, consts, w1, w2, td1, td2, mats, out):
    with ExitStack() as ctx:
        def sb(name, shape, dt=F32):
            return ctx.enter_context(nc.sbuf_tensor(name, shape, dt))

        def bank(name):
            return ctx.enter_context(nc.psum_tensor(name, [P, HALVES * L], F32))

        def sem(name):
            return ctx.enter_context(nc.semaphore(name))

        vec_sb = sb("vec_sb", [P, len(VECS), HALVES])
        const_sb = sb("const_sb", [P, consts.shape[1]])
        ident = const_sb[:, 0:P]
        spread = const_sb[:, P:P + CHUNKS * P].rearrange("p (c m) -> p c m", m=P)
        gather = const_sb[:, P * (1 + CHUNKS):P * (1 + CHUNKS) + HALVES * H].rearrange("p (a h) -> p a h", h=H)
        mean_at = P * (1 + CHUNKS) + HALVES * H
        head_mean = const_sb[:, mean_at:mean_at + P]
        head_mean_row = const_sb[:, mean_at + P:mean_at + P + H]
        unblock = const_sb[:, mean_at + P + H:].rearrange("p (b m) -> p b m", m=P)
        spread_r = sb("spread_r", [P, CHUNKS, P], F32R)
        bonus = sb("bonus", [P, HALVES, G, H])
        w1_sb = sb("w1_sb", [P, HALVES, NMIX * DM])
        w2_sb = sb("w2_sb", [P, NMIX, E])
        td1_sb = sb("td1_sb", [P, HALVES, DD])
        td2_sb = sb("td2_sb", [P, E])
        W = {m: sb(f"{m}_sb", [P, HALVES, E]) for m in MATS}
        state_rows = sb("state_rows", [B, 2, E])
        s0 = sb("s0", [P, HALVES, B, S])
        eps = sb("eps", [P, 1])

        x_sb = sb("x_sb", [P, B, TILES, E])
        xc = sb("xc", [P, B, HALVES, L + 1])
        k_sb = sb("k_sb", [P, B, HALVES, L])
        v_sb = sb("v_sb", [P, B, Q, L])
        g_sb = sb("g_sb", [P, B, Q, L])
        decay = sb("decay", [P, B, HALVES, Q, L])
        y_sb = sb("y_sb", [P, B, TILES, E])

        stats1 = sb("stats1", [P, B * TILES, 6])
        mv1 = sb("mv1", [P, B * TILES, 2])
        std1 = sb("std1", [P, B * TILES])
        rstd1 = sb("rstd1", [P, B * TILES])
        shift_1 = sb("shift_1", [P, B * TILES])
        xn = sb("xn", [P, TILES, E])
        xa = sb("xa", [P, HALVES, L + 1])
        before = sb("before", [P, B, HALVES])
        r_sb = sb("r_sb", [P, HALVES, L])
        sx = sb("sx", [P, HALVES, L])
        xin = sb("xin", [P, HALVES, L])
        lora = sb("lora", [P, 2, L])
        td_hid = sb("td_hid", [P, L])
        xm = [sb(f"xm{j}", [P, HALVES, L]) for j in range(NMIX)]
        v_hi = sb("v_hi", [P, Q, L], F32R)
        v_lo = sb("v_lo", [P, Q, L], F32R)
        th_g = sb("th_g", [P, Q, L])
        ed = sb("ed", [P, HALVES, L])

        rec = sb("rec", [P, CHUNKS, Q, L])
        rk = sb("rk", [P, HALVES, L])
        vr = sb("vr", [P, Q, L])
        o_sb = sb("o_sb", [P, Q, L])
        cen = sb("cen", [P, Q, L])
        sq = sb("sq", [P, Q, L])
        std_o = sb("std_o", [P, TB])
        rstd_o = sb("rstd_o", [P, TB])
        on = sb("on", [P, Q, L])
        gated = sb("gated", [P, Q, L])

        x1 = sb("x1", [P, TILES, E])
        stats2 = sb("stats2", [P, TILES, 6])
        mdiff2, within2, msum2, between2, mean2, esq2 = (sb(n, [P, TILES]) for n in (
            "mdiff2", "within2", "msum2", "between2", "mean2", "esq2"))
        std2 = sb("std2", [P, TILES])
        rstd2 = sb("rstd2", [P, TILES])
        xn2 = sb("xn2", [P, TILES, E])
        sx2 = sb("sx2", [P, HALVES, L])
        xk2 = sb("xk2", [P, HALVES, L])
        xr2 = sb("xr2", [P, HALVES, L])
        relu = sb("relu", [P, HALVES, L])
        kk = sb("kk", [P, HALVES, L])
        th_r = sb("th_r", [P, TILES, E])
        f1 = sb("f1", [P, TILES, E])

        pa = [bank(f"pa{i}") for i in range(3)]
        pv = [bank(f"pv{i}") for i in range(2)]
        py = bank("py")
        pc = [bank(f"pc{i}") for i in range(2)]

        def by2(b):
            return b[:].rearrange("p (a t) -> p a t", a=2)

        def vcol(name, a):
            return vec_sb[:, VECS.index(name), a:a + 1]

        x_in, vec_in, const_in, state_in, w_in = (sem(n) for n in ("x_in", "vec_in", "const_in", "state_in", "w_in"))
        w1_in, w2_in, td_in, out_done = (sem(n) for n in ("w1_in", "w2_in", "td_in", "out_done"))
        mat_in = {m: sem(f"{m}_in") for m in MATS}
        zeroed, stats1_ready, mv1_ready, std1_ready, rstd1_ready = (sem(n) for n in (
            "zeroed", "stats1_ready", "mv1_ready", "std1_ready", "rstd1_ready"))
        state_tr_done, state_cols_ready, bonus_ready, spread_ready = (sem(n) for n in (
            "state_tr_done", "state_cols_ready", "bonus_ready", "spread_ready"))
        xn_ready, sx_ready, xin_ready, m_ready, g_ready = (sem(n) for n in (
            "xn_ready", "sx_ready", "xin_ready", "m_ready", "g_ready"))
        a_ready, scan_done, vr_ready, o_ready, cen_ready, rstdo_ready = (sem(n) for n in (
            "a_ready", "scan_done", "vr_ready", "o_ready", "cen_ready", "rstdo_ready"))
        on_ready, gated_ready, x1_ready, stats2_ready, mv2_ready, rstd2_ready = (sem(n) for n in (
            "on_ready", "gated_ready", "x1_ready", "stats2_ready", "mv2_ready", "rstd2_ready"))
        xn2_ready, xk2_ready, xr2_ready, f1_ready, y_ready = (sem(n) for n in (
            "xn2_ready", "xk2_ready", "xr2_ready", "f1_ready", "y_ready"))
        mdiff_ready, between_ready = sem("mdiff_ready"), sem("between_ready")
        xa_ready, lora_ready, tdh_ready, k_ready, v_ready, r_ready, thg_ready, ed_ready, w_ready = (sem(n) for n in (
            "xa_ready", "lora_ready", "tdh_ready", "k_ready", "v_ready", "r_ready", "thg_ready", "ed_ready",
            "w_ready"))
        sq_ready, stdo_ready, std2_ready, xc_ready, relu_ready, kk_ready, thr_ready = (sem(n) for n in (
            "sq_ready", "stdo_ready", "std2_ready", "xc_ready", "relu_ready", "kk_ready", "thr_ready"))
        xm_ready, s0_placed, p_ready, rk_ready, sx2_ready = (sem(n) for n in (
            "xm_ready", "s0_placed", "p_ready", "rk_ready", "sx2_ready"))
        vlo_ready, vhi_ready = sem("vlo_ready"), sem("vhi_ready")
        tr1_done, w1_done, w2_done, td1_done, td2_done, pk_done, pvv_done, pr_done, pg_done = (sem(n) for n in (
            "tr1_done", "w1_done", "w2_done", "td1_done", "td2_done", "pk_done", "pvv_done", "pr_done",
            "pg_done"))
        spread_done, gather_done, bonus_done, mean_done, var_done, unblock_done = (sem(n) for n in (
            "spread_done", "gather_done", "bonus_done", "mean_done", "var_done", "unblock_done"))
        wo_done, tr2_done, fk_done, fr_done, fv_done = (sem(n) for n in (
            "wo_done", "tr2_done", "fk_done", "fr_done", "fv_done"))

        block = ctx.enter_context(nc.Block())

        @block.sync
        def _(sp):
            sp.dma_start(x_sb[:], x.rearrange("b (t p) e -> p b t e", p=P)).then_inc(x_in, 16)
            sp.dma_start(vec_sb[:], vecs).then_inc(vec_in, 16)
            sp.dma_start(state_rows[:], state[:, 0:2, :]).then_inc(state_in, 16)
            sp.dma_start(const_sb[:], consts).then_inc(const_in, 16)
            sp.wait_ge(zeroed, 2)
            for j in range(NMIX):
                row = DM * (j % G)
                sp.dma_start(w2_sb[row:row + DM, j, :], w2[j]).then_inc(w2_in, 16)
            sp.dma_start(td1_sb[:], td1.rearrange("(a p) n -> p a n", p=P)).then_inc(td_in, 16)
            sp.dma_start(td2_sb[0:DD, :], td2).then_inc(td_in, 16)
            for m in ("Wv", "Wg", "Wfk", "Wfv"):
                sp.dma_start(W[m][:], mats[m].rearrange("(a p) n -> p a n", p=P)).then_inc(mat_in[m], 16)
            with sp.Fori(0, B) as b:
                sp.wait_ge(y_ready, b + 1)
                sp.dma_start(out[b].rearrange("(t p) e -> p t e", p=P), y_sb[:, b]).then_inc(out_done, 16)
            sp.wait_ge(out_done, 16 * B)

        @block.gpsimd
        def _(pool):
            def s0_place(b):
                if not isinstance(b, int) or b:
                    pool.wait_ge(gather_done, 2 * b)
                for a in range(HALVES):
                    dst = rec[:, G * a:G * a + G, :, 0]
                    src = s0[:, a, b, :].rearrange("p (q g) -> p g q", g=G)
                    nc.gpsimd.tensor_copy(dst, src).then_inc(s0_placed, 1)

            def product(b, c):
                if c == 0:
                    pool.wait_ge(r_ready, b + 1)
                pool.wait_ge(scan_done, CHUNKS * b + c + 1)
                r_b = r_sb[:, c // G, :].unsqueeze(1).broadcast_to([P, Q, L])
                nc.gpsimd.tensor_tensor(rec[:, c], rec[:, c], r_b, ALU.mult).then_inc(p_ready, 1)

            def mixed(n, i):
                j = MIX_ORDER[i]
                pool.wait_ge(m_ready, 10 * n + 2 * i + 2)
                nc.gpsimd.tensor_tensor(xm[j][:], xm[j][:], xa[:, :, 1:L + 1], ALU.add).then_inc(xm_ready, 1)

            def rk_product(b):
                pool.wait_ge(k_ready, b + 1)
                pool.wait_ge(r_ready, b + 1)
                if not isinstance(b, int) or b:
                    pool.wait_ge(bonus_done, b)
                nc.gpsimd.tensor_tensor(rk[:], r_sb[:], k_sb[:, b], ALU.mult).then_inc(rk_ready, 1)

            def shift2(b):
                pool.wait_ge(xc_ready, 2 * b + 2)
                nc.gpsimd.tensor_tensor(sx2[:], xc[:, b, :, 0:L], xc[:, b, :, 1:L + 1],
                                        ALU.subtract).then_inc(sx2_ready, 1)

            def v_low(n):
                pool.wait_ge(vhi_ready, n + 1)
                pool.wait_ge(v_ready, n + 1)
                nc.gpsimd.tensor_tensor(v_lo[:], v_sb[:, n], v_hi[:].bitcast(F32), ALU.subtract).then_inc(vlo_ready, 1)

            def round_(a, b, c):
                if b is not None:
                    s0_place(b)
                    rk_product(b)
                    product(b, 0)
                    product(b, 1)
                if a is not None:
                    mixed(a, 0)
                    mixed(a, 1)
                    mixed(a, 2)
                if b is not None:
                    product(b, 2)
                if a is not None:
                    mixed(a, 3)
                if b is not None:
                    product(b, 3)
                if a is not None:
                    mixed(a, 4)
                if c is not None:
                    shift2(c)
                if b is not None:
                    product(b, 4)
                    product(b, 5)
                    product(b, 6)
                    product(b, 7)
                if a is not None:
                    v_low(a)

            nc.gpsimd.memset(w2_sb[:], 0.0).then_inc(zeroed, 1)
            nc.gpsimd.memset(td2_sb[:], 0.0).then_inc(zeroed, 1)
            nc.gpsimd.memset(lora[:], 0.0).then_inc(zeroed, 1)
            nc.gpsimd.memset(td_hid[:], 0.0).then_inc(zeroed, 1)
            nc.gpsimd.memset(decay[:, :, :, :, 0], 0.0).then_inc(zeroed, 1)
            nc.gpsimd.memset(eps[:], EPS).then_inc(zeroed, 1)
            pool.wait_ge(state_in, 48)
            round_(0, None, None)
            round_(1, 0, None)
            with pool.Fori(1, B - 1) as i:
                round_(i + 1, i, i - 1)
            round_(None, B - 1, B - 2)
            round_(None, None, B - 1)

        @block.scalar
        def _(act):
            act.dma_start(w1_sb[:], w1.rearrange("(a p) n -> p a n", p=P)).then_inc(w1_in, 16)
            for m in ("Wk", "Wr", "Wo", "Wfr"):
                act.dma_start(W[m][:], mats[m].rearrange("(a p) n -> p a n", p=P)).then_inc(mat_in[m], 16)
            s0_rows = state.rearrange("b r e -> b (r e)")[:, 2 * E:(2 + S) * E]
            for a in range(HALVES):
                half = s0_rows[:, a * P * S:(a + 1) * P * S]
                act.dma_start(s0[:, a], half.rearrange("b (p j) -> p b j", j=S)).then_inc(state_in, 16)

            def normalise1(n):
                if not isinstance(n, int) or n:
                    act.wait_ge(tr1_done, n)
                for t in range(TILES):
                    i = bass.ds(n * TILES + t, 1)
                    nc.scalar.activation(xn[:, t, :], x_sb[:, n, t, :], ACT.Identity, bias=shift_1[:, i],
                                         scale=rstd1[:, i]).then_inc(xn_ready, 1)

            def norm1(n):
                act.wait_ge(tr1_done, n + 1)
                if not isinstance(n, int) or n:
                    act.wait_ge(xm_ready, NMIX * n)
                nc.scalar.activation(xa[:, :, 0], before[:, n, :], ACT.Copy).then_inc(xa_ready, 1)
                for a in range(HALVES):
                    nc.scalar.activation(xa[:, a, 1:L + 1], pa[0][:, a * L:(a + 1) * L], ACT.Identity,
                                         bias=vcol("ln1_b", a), scale=vcol("ln1_w", a)).then_inc(xa_ready, 1)

            def lora_tanh(n):
                act.wait_ge(w1_done, n + 1)
                if not isinstance(n, int) or n:
                    act.wait_ge(w2_done, 5 * n)
                nc.scalar.activation(lora[:, 0, :], pa[1][:, 0:L], ACT.Tanh).then_inc(lora_ready, 1)
                nc.scalar.activation(lora[0:DM, 1, :], pa[1][0:DM, L:2 * L], ACT.Tanh).then_inc(lora_ready, 1)

            def td_tanh(n):
                act.wait_ge(td1_done, n + 1)
                nc.scalar.activation(td_hid[0:DD, :], pa[2][0:DD, 0:L], ACT.Tanh).then_inc(tdh_ready, 1)

            def take_k(n):
                act.wait_ge(pk_done, n + 1)
                nc.scalar.activation(k_sb[:, n], by2(pa[1]), ACT.Copy).then_inc(k_ready, 1)

            def take_v(n):
                act.wait_ge(pvv_done, n + 1)
                if not isinstance(n, int) or n:
                    act.wait_ge(spread_done, CHUNKS * n)
                nc.scalar.activation(v_hi[:], by2(pa[1]), ACT.Copy).then_inc(vhi_ready, 1)
                nc.scalar.activation(v_sb[:, n], by2(pa[1]), ACT.Copy).then_inc(v_ready, 1)

            def take_r(n):
                act.wait_ge(pr_done, n + 1)
                if not isinstance(n, int) or n:
                    act.wait_ge(p_ready, CHUNKS * n)
                nc.scalar.activation(r_sb[:], by2(pa[2]), ACT.Copy).then_inc(r_ready, 1)

            def decays(n):
                act.wait_ge(td2_done, n + 1)
                if not isinstance(n, int) or n:
                    act.wait_ge(w_ready, 2 * n)
                for a in range(HALVES):
                    nc.scalar.activation(ed[:, a, :], pa[2][:, a * L:(a + 1) * L], ACT.Exp,
                                         bias=vcol("time_decay", a)).then_inc(ed_ready, 1)
                act.wait_ge(ed_ready, 2 * n + 2)
                for q in range(Q):
                    nc.scalar.activation(decay[:, n, :, q, 1:L], ed[:, :, 0:L - 1], ACT.Exp,
                                         scale=-1.0).then_inc(w_ready, 1)

            def gate_tanh(n):
                act.wait_ge(pg_done, n + 1)
                nc.scalar.activation(th_g[:], by2(pa[0]), ACT.Tanh, scale=0.5).then_inc(thg_ready, 1)

            def squares(b):
                act.wait_ge(cen_ready, b + 1)
                nc.scalar.activation(sq[:], cen[:], ACT.Square).then_inc(sq_ready, 1)

            def head_std(b):
                act.wait_ge(var_done, b + 1)
                nc.scalar.activation(std_o[:], pc[0][:, 0:TB], ACT.Sqrt, bias=eps[:]).then_inc(stdo_ready, 1)

            def token_std(b):
                act.wait_ge(mv2_ready, b + 1)
                nc.scalar.activation(std2[:], esq2[:], ACT.Sqrt, bias=eps[:], scale=1.0 / E).then_inc(std2_ready, 1)

            def norm2(b):
                act.wait_ge(tr2_done, b + 1)
                for a in range(HALVES):
                    nc.scalar.activation(xc[:, b, a, 1:L + 1], pc[1][:, a * L:(a + 1) * L], ACT.Identity,
                                         bias=vcol("ln2_b", a), scale=vcol("ln2_w", a)).then_inc(xc_ready, 1)

            def relu_squared(b):
                act.wait_ge(fk_done, b + 1)
                nc.scalar.activation(relu[:], by2(pc[0]), ACT.Relu).then_inc(relu_ready, 1)
                act.wait_ge(relu_ready, b + 1)
                nc.scalar.activation(kk[:], relu[:], ACT.Square).then_inc(kk_ready, 1)

            def receptance_tanh(b):
                act.wait_ge(fr_done, b + 1)
                nc.scalar.activation(th_r[:], by2(pc[1]), ACT.Tanh, scale=0.5).then_inc(thr_ready, 1)

            def round_(a, b, c):
                if a is not None:
                    normalise1(a)
                    norm1(a)
                if c is not None:
                    squares(c)
                if a is not None:
                    lora_tanh(a)
                if c is not None:
                    head_std(c)
                if a is not None:
                    take_k(a)
                if c is not None:
                    token_std(c)
                if a is not None:
                    td_tanh(a)
                if c is not None:
                    norm2(c)
                if a is not None:
                    decays(a)
                if c is not None:
                    relu_squared(c)
                if a is not None:
                    gate_tanh(a)
                    take_v(a)
                if c is not None:
                    receptance_tanh(c)
                if a is not None:
                    take_r(a)

            act.wait_ge(mv1_ready, B * TILES)
            act.wait_ge(zeroed, 6)
            nc.scalar.activation(std1[:], mv1[:, :, 1], ACT.Sqrt, bias=eps[:]).then_inc(std1_ready, 1)
            act.wait_ge(state_tr_done, 1)
            rows = pc[0][:, 0:2 * 2 * B].rearrange("p (a r b) -> p b a r", a=HALVES, r=2)
            nc.scalar.activation(before[:], rows[:, :, :, 1], ACT.Copy).then_inc(state_cols_ready, 1)
            nc.scalar.activation(xc[:, :, :, 0], rows[:, :, :, 0], ACT.Copy).then_inc(state_cols_ready, 1)
            act.wait_ge(vec_in, 16)
            act.wait_ge(rstd1_ready, 2)
            round_(0, None, None)
            round_(1, 0, None)
            with act.Fori(1, B - 1) as i:
                round_(i + 1, i, i - 1)
            round_(None, B - 1, B - 2)
            round_(None, None, B - 1)

        @block.vector
        def _(dve):
            def shift1(n):
                dve.wait_ge(xa_ready, 3 * n + 3)
                nc.vector.tensor_tensor(sx[:], xa[:, :, 0:L], xa[:, :, 1:L + 1],
                                        ALU.subtract).then_inc(sx_ready, 1)
                dve.wait_ge(sx_ready, n + 1)
                for a in range(HALVES):
                    nc.vector.scalar_tensor_tensor(xin[:, a, :], sx[:, a, :], vcol("maa_x", a), xa[:, a, 1:L + 1],
                                                   ALU.mult, ALU.add).then_inc(xin_ready, 1)

            def mix(n, i):
                j = MIX_ORDER[i]
                src = pa[(0, 1, 2, 0, 0)[i]]
                dve.wait_ge(w2_done, 5 * n + i + 1)
                for a in range(HALVES):
                    nc.vector.scalar_tensor_tensor(xm[j][:, a, :], src[:, a * L:(a + 1) * L], vcol(f"maa{j}", a),
                                                   sx[:, a, :], ALU.add, ALU.mult).then_inc(m_ready, 1)

            def gate(n):
                dve.wait_ge(thg_ready, n + 1)
                nc.vector.scalar_tensor_tensor(g_sb[:, n], th_g[:], 1.0, by2(pa[0]), ALU.add,
                                               ALU.mult).then_inc(g_ready, 1)

            def kv(b, c):
                if c == 0:
                    dve.wait_ge(k_ready, b + 1)
                    dve.wait_ge(s0_placed, 2 * b + 2)
                dve.wait_ge(spread_done, CHUNKS * b + c + 1)
                k_b = k_sb[:, b, c // G, 0:L - 1].unsqueeze(1).broadcast_to([P, Q, L - 1])
                nc.vector.tensor_tensor(rec[:, c, :, 1:L], by2(pv[c % 2])[:, :, 0:L - 1], k_b,
                                        ALU.mult).then_inc(a_ready, 1)

            def scan(b, c):
                if c == 0:
                    dve.wait_ge(w_ready, 2 * b + 2)
                dve.wait_ge(a_ready, CHUNKS * b + c + 1)
                rows = rec[:, c].rearrange("p q t -> p (q t)")
                nc.vector.tensor_tensor_scan(rows, decay[:, b, c // G].rearrange("p q t -> p (q t)"), rows, 0.0,
                                             ALU.mult, ALU.add).then_inc(scan_done, 1)

            def bonus_out(b):
                dve.wait_ge(bonus_done, b + 1)
                rb = pv[0][:, 0:L].unsqueeze(1).broadcast_to([P, Q, L])
                nc.vector.tensor_tensor(vr[:], rb, v_sb[:, b], ALU.mult).then_inc(vr_ready, 1)

            def wkv_out(b):
                dve.wait_ge(gather_done, 2 * b + 2)
                dve.wait_ge(vr_ready, b + 1)
                nc.vector.tensor_tensor(o_sb[:], by2(py), vr[:], ALU.add).then_inc(o_ready, 1)

            def centre(b):
                dve.wait_ge(mean_done, b + 1)
                mean = pc[1][:, 0:L].unsqueeze(1).broadcast_to([P, Q, L])
                nc.vector.tensor_tensor(cen[:], o_sb[:], mean, ALU.subtract).then_inc(cen_ready, 1)

            def head_rstd(b):
                dve.wait_ge(stdo_ready, b + 1)
                nc.vector.reciprocal(rstd_o[:], std_o[:]).then_inc(rstdo_ready, 1)

            def gated_norm(b):
                dve.wait_ge(unblock_done, b + 1)
                for q in range(Q):
                    nc.vector.scalar_tensor_tensor(on[:, q, :], cen[:, q, :], vcol("gn_w", q), pc[1][:, 0:L], ALU.mult,
                                                   ALU.mult).then_inc(on_ready, 1)
                for q in range(Q):
                    dve.wait_ge(on_ready, 2 * b + q + 1)
                    nc.vector.scalar_tensor_tensor(gated[:, q, :], on[:, q, :], vcol("gn_b", q), g_sb[:, b, q, :],
                                                   ALU.add, ALU.mult).then_inc(gated_ready, 1)

            def residual(b):
                dve.wait_ge(wo_done, b + 1)
                nc.vector.scalar_tensor_tensor(x1[:], by2(pc[0]), 0.5, x_sb[:, b], ALU.mult,
                                               ALU.add).then_inc(x1_ready, 1)
                dve.wait_ge(x1_ready, b + 1)
                for t in range(TILES):
                    nc.vector.bn_stats(stats2[:, t, :], x1[:, t, :]).then_inc(stats2_ready, 1)
                dve.wait_ge(stats2_ready, 2 * b + 2)
                nc.vector.tensor_tensor(mdiff2[:], stats2[:, :, 1], stats2[:, :, 4], ALU.subtract).then_inc(mdiff_ready, 1)
                nc.vector.tensor_tensor(within2[:], stats2[:, :, 2], stats2[:, :, 5], ALU.add).then_inc(mdiff_ready, 1)
                nc.vector.tensor_tensor(msum2[:], stats2[:, :, 1], stats2[:, :, 4], ALU.add).then_inc(mdiff_ready, 1)
                dve.wait_ge(mdiff_ready, 3 * b + 3)
                nc.vector.tensor_tensor(between2[:], mdiff2[:], mdiff2[:], ALU.mult).then_inc(between_ready, 1)
                nc.vector.tensor_scalar(mean2[:], msum2[:], 0.5, None, ALU.mult).then_inc(between_ready, 1)
                dve.wait_ge(between_ready, 2 * b + 2)
                nc.vector.scalar_tensor_tensor(esq2[:], between2[:], E / 4, within2[:], ALU.mult,
                                               ALU.add).then_inc(mv2_ready, 1)

            def normalise2(b):
                dve.wait_ge(std2_ready, b + 1)
                nc.vector.reciprocal(rstd2[:], std2[:]).then_inc(rstd2_ready, 1)
                dve.wait_ge(rstd2_ready, b + 1)
                for t in range(TILES):
                    nc.vector.tensor_scalar(xn2[:, t, :], x1[:, t, :], mean2[:, t:t + 1], rstd2[:, t:t + 1],
                                            ALU.subtract, ALU.mult).then_inc(xn2_ready, 1)

            def mix2(b):
                dve.wait_ge(sx2_ready, b + 1)
                for name, dst, ready in (("ffn_maa_k", xk2, xk2_ready), ("ffn_maa_r", xr2, xr2_ready)):
                    for a in range(HALVES):
                        nc.vector.scalar_tensor_tensor(dst[:, a, :], sx2[:, a, :], vcol(name, a),
                                                       xc[:, b, a, 1:L + 1], ALU.mult, ALU.add).then_inc(ready, 1)

            def finish(b):
                dve.wait_ge(thr_ready, b + 1)
                dve.wait_ge(fv_done, b + 1)
                nc.vector.scalar_tensor_tensor(f1[:], th_r[:], 1.0, by2(pc[0]), ALU.add, ALU.mult).then_inc(f1_ready, 1)
                dve.wait_ge(f1_ready, b + 1)
                nc.vector.scalar_tensor_tensor(y_sb[:, b], f1[:], 0.5, x1[:], ALU.mult, ALU.add).then_inc(y_ready, 1)

            def round_(a, b, c):
                if b is not None:
                    kv(b, 0)
                if a is not None:
                    shift1(a)
                if c is not None:
                    centre(c)
                if b is not None:
                    kv(b, 1)
                    scan(b, 0)
                    kv(b, 2)
                    scan(b, 1)
                if a is not None:
                    mix(a, 0)
                if c is not None:
                    head_rstd(c)
                if a is not None:
                    mix(a, 1)
                if b is not None:
                    scan(b, 2)
                if c is not None:
                    gated_norm(c)
                if a is not None:
                    mix(a, 2)
                    mix(a, 3)
                if b is not None:
                    kv(b, 3)
                    scan(b, 3)
                    kv(b, 4)
                if c is not None:
                    residual(c)
                    normalise2(c)
                if a is not None:
                    mix(a, 4)
                if b is not None:
                    kv(b, 5)
                    scan(b, 4)
                    kv(b, 6)
                    scan(b, 5)
                if c is not None:
                    mix2(c)
                if b is not None:
                    scan(b, 6)
                    kv(b, 7)
                    scan(b, 7)
                if a is not None:
                    gate(a)
                if b is not None:
                    bonus_out(b)
                    wkv_out(b)
                if c is not None:
                    finish(c)

            dve.wait_ge(x_in, 16)
            for i in range(B * TILES):
                nc.vector.bn_stats(stats1[:, i, :], x_sb[:, i // TILES, i % TILES, :]).then_inc(stats1_ready, 1)
            for i in range(B * TILES):
                dve.wait_ge(stats1_ready, i + 1)
                nc.vector.bn_aggr(mv1[:, i, :], stats1[:, i, :]).then_inc(mv1_ready, 1)
            dve.wait_ge(std1_ready, 1)
            nc.vector.reciprocal(rstd1[:], std1[:]).then_inc(rstd1_ready, 1)
            dve.wait_ge(rstd1_ready, 1)
            nc.vector.scalar_tensor_tensor(shift_1[:], mv1[:, :, 0], -1.0, rstd1[:], ALU.mult,
                                           ALU.mult).then_inc(rstd1_ready, 1)
            dve.wait_ge(vec_in, 16)
            dve.wait_ge(const_in, 16)
            for a in range(HALVES):
                g_b = gather[:, a, :].unsqueeze(1).broadcast_to([P, G, H])
                nc.vector.tensor_scalar(bonus[:, a], g_b, vcol("u", a), None, ALU.mult).then_inc(bonus_ready, 1)
            nc.vector.tensor_copy(spread_r[:], spread).then_inc(spread_ready, 1)
            dve.wait_ge(state_cols_ready, 2)
            round_(0, None, None)
            round_(1, 0, None)
            with dve.Fori(1, B - 1) as i:
                round_(i + 1, i, i - 1)
            round_(None, B - 1, B - 2)
            round_(None, None, B - 1)

        @block.tensor
        def _(pe):
            def two_halves(dst, w, rhs, m=P, cols=HALVES):
                for o in range(cols):
                    for a in range(HALVES):
                        mm = nc.tensor.matmul(dst[0:m, o * L:(o + 1) * L], w[:, a, o * m:(o + 1) * m], rhs[:, a, :],
                                              start=(a == 0), stop=(a == HALVES - 1))
                return mm

            def token_major(dst, act_t, w):
                for t in range(TILES):
                    for a in range(HALVES):
                        mm = nc.tensor.matmul(dst[:, t * E:(t + 1) * E], act_t[:, a, t * P:(t + 1) * P], w[:, a, :],
                                              start=(a == 0), stop=(a == HALVES - 1))
                return mm

            def transposes(dst, src, done):
                for a in range(HALVES):
                    for t in range(TILES):
                        mm = nc.tensor.transpose(dst[:, a * L + t * P:a * L + (t + 1) * P],
                                                 src[:, t, a * P:(a + 1) * P], ident)
                mm.then_inc(done, 1)

            def tr1(n):
                pe.wait_ge(xn_ready, 2 * n + 2)
                if not isinstance(n, int) or n:
                    pe.wait_ge(g_ready, n)
                transposes(pa[0], xn, tr1_done)

            def lora_in(n):
                pe.wait_ge(xin_ready, 2 * n + 2)
                if not isinstance(n, int) or n:
                    pe.wait_ge(v_ready, n)
                for a in range(HALVES):
                    nc.tensor.matmul(pa[1][:, 0:L], w1_sb[:, a, 0:P], xin[:, a, :], start=(a == 0),
                                     stop=(a == HALVES - 1))
                for a in range(HALVES):
                    mm = nc.tensor.matmul(pa[1][0:DM, L:2 * L], w1_sb[:, a, P:P + DM], xin[:, a, :],
                                          start=(a == 0), stop=(a == HALVES - 1))
                mm.then_inc(w1_done, 1)

            def lora_out(n, i):
                j = MIX_ORDER[i]
                if i == 0:
                    pe.wait_ge(lora_ready, 2 * n + 2)
                elif i == 2 and (not isinstance(n, int) or n):
                    pe.wait_ge(r_ready, n)
                elif i == 3:
                    pe.wait_ge(m_ready, 10 * n + 2)
                elif i == 4:
                    pe.wait_ge(m_ready, 10 * n + 8)
                dst = pa[(0, 1, 2, 0, 0)[i]]
                for o in range(HALVES):
                    mm = nc.tensor.matmul(dst[:, o * L:(o + 1) * L], w2_sb[:, j, o * P:(o + 1) * P],
                                          lora[:, j // G, :], start=True, stop=True)
                mm.then_inc(w2_done, 1)

            def td_in_(n):
                pe.wait_ge(xm_ready, 5 * n + 3)
                two_halves(pa[2], td1_sb, xm[MIX_W], m=DD, cols=1).then_inc(td1_done, 1)

            def td_out(n):
                pe.wait_ge(tdh_ready, n + 1)
                for o in range(HALVES):
                    mm = nc.tensor.matmul(pa[2][:, o * L:(o + 1) * L], td2_sb[:, o * P:(o + 1) * P], td_hid[:],
                                          start=True, stop=True)
                mm.then_inc(td2_done, 1)

            def project_k(n):
                pe.wait_ge(m_ready, 10 * n + 4)
                pe.wait_ge(xm_ready, 5 * n + 1)
                two_halves(pa[1], W["Wk"], xm[MIX_K]).then_inc(pk_done, 1)

            def project_v(n):
                pe.wait_ge(k_ready, n + 1)
                pe.wait_ge(xm_ready, 5 * n + 2)
                two_halves(pa[1], W["Wv"], xm[MIX_V]).then_inc(pvv_done, 1)

            def project_r(n):
                pe.wait_ge(ed_ready, 2 * n + 2)
                pe.wait_ge(xm_ready, 5 * n + 4)
                two_halves(pa[2], W["Wr"], xm[MIX_R]).then_inc(pr_done, 1)

            def project_g(n):
                pe.wait_ge(xm_ready, 5 * n + 5)
                two_halves(pa[0], W["Wg"], xm[MIX_G]).then_inc(pg_done, 1)

            def spread_v(b, c):
                if c == 0:
                    pe.wait_ge(vlo_ready, b + 1)
                    if not isinstance(b, int) or b:
                        pe.wait_ge(vr_ready, b)
                elif c >= 2:
                    pe.wait_ge(a_ready, CHUNKS * b + c - 1)
                for part, v in enumerate((v_hi, v_lo)):
                    mm = nc.tensor.matmul(pv[c % 2][:], spread_r[:, c, :], v[:].rearrange("p q t -> p (q t)"),
                                          start=(part == 0), stop=(part == 1))
                mm.then_inc(spread_done, 1)

            def gather_half(b, a):
                pe.wait_ge(p_ready, CHUNKS * b + G * (a + 1))
                if a == 0 and (not isinstance(b, int) or b):
                    pe.wait_ge(o_ready, b)
                for g in range(G):
                    mm = nc.tensor.matmul(py[H * g:H * (g + 1), :], gather[:, a, :],
                                          rec[:, G * a + g].rearrange("p q t -> p (q t)"), start=(a == 0),
                                          stop=(a == HALVES - 1))
                mm.then_inc(gather_done, 1)

            def bonus_sum(b):
                pe.wait_ge(rk_ready, b + 1)
                pe.wait_ge(a_ready, CHUNKS * b + CHUNKS - 1)
                for a in range(HALVES):
                    mm = nc.tensor.matmul(pv[0][:, 0:L], bonus[:, a].rearrange("p g h -> p (g h)"), rk[:, a, :],
                                          start=(a == 0), stop=(a == HALVES - 1))
                mm.then_inc(bonus_done, 1)

            def head_sum(dst, src, done):
                for q in range(Q):
                    mm = nc.tensor.matmul(dst[:, 0:L], head_mean, src[:, q, :], start=(q == 0), stop=(q == Q - 1))
                mm.then_inc(done, 1)

            def mean_(b):
                pe.wait_ge(o_ready, b + 1)
                if isinstance(b, int) and b:
                    pe.wait_ge(thr_ready, b)
                head_sum(pc[1], o_sb, mean_done)

            def var_(b):
                pe.wait_ge(sq_ready, b + 1)
                for q in range(Q):
                    for tb in range(G):
                        mm = nc.tensor.matmul(pc[0][H * tb:H * (tb + 1), 0:TB], head_mean_row,
                                              sq[:, q, tb * TB:(tb + 1) * TB], start=(q == 0), stop=(q == Q - 1))
                mm.then_inc(var_done, 1)

            def unblock_rstd(b):
                pe.wait_ge(rstdo_ready, b + 1)
                for tb in range(G):
                    mm = nc.tensor.matmul(pc[1][:, tb * TB:(tb + 1) * TB], unblock[:, tb, :], rstd_o[:], start=True,
                                          stop=True)
                mm.then_inc(unblock_done, 1)

            def out_product(b):
                pe.wait_ge(gated_ready, 2 * b + 2)
                token_major(pc[0], gated, W["Wo"]).then_inc(wo_done, 1)

            def tr2(b):
                pe.wait_ge(xn2_ready, 2 * b + 2)
                transposes(pc[1], xn2, tr2_done)

            def ffn_k(b):
                pe.wait_ge(xk2_ready, 2 * b + 2)
                two_halves(pc[0], W["Wfk"], xk2).then_inc(fk_done, 1)

            def ffn_r(b):
                pe.wait_ge(xr2_ready, 2 * b + 2)
                token_major(pc[1], xr2, W["Wfr"]).then_inc(fr_done, 1)

            def ffn_v(b):
                pe.wait_ge(kk_ready, b + 1)
                token_major(pc[0], kk, W["Wfv"]).then_inc(fv_done, 1)

            def round_(a, b, c, first=False):
                if a is not None:
                    tr1(a)
                if b is not None:
                    spread_v(b, 0)
                if c is not None:
                    mean_(c)
                if b is not None:
                    spread_v(b, 1)
                    spread_v(b, 2)
                if a is not None:
                    if first:
                        pe.wait_ge(w1_in, 16)
                    lora_in(a)
                if b is not None:
                    spread_v(b, 3)
                if c is not None:
                    var_(c)
                if a is not None:
                    if first:
                        pe.wait_ge(w2_in, 16 * NMIX)
                        pe.wait_ge(td_in, 32)
                        pe.wait_ge(zeroed, 6)
                    lora_out(a, 0)
                    lora_out(a, 1)
                if b is not None:
                    spread_v(b, 4)
                if a is not None:
                    lora_out(a, 2)
                if c is not None:
                    unblock_rstd(c)
                if a is not None:
                    lora_out(a, 3)
                    if first:
                        for m in MATS:
                            pe.wait_ge(mat_in[m], 16)
                        pe.wait_ge(spread_ready, 1)
                    project_k(a)
                if c is not None:
                    out_product(c)
                if b is not None:
                    spread_v(b, 5)
                if a is not None:
                    lora_out(a, 4)
                    td_in_(a)
                    project_v(a)
                if b is not None:
                    spread_v(b, 6)
                    gather_half(b, 0)
                if c is not None:
                    tr2(c)
                if a is not None:
                    td_out(a)
                if b is not None:
                    spread_v(b, 7)
                if a is not None:
                    project_g(a)
                    project_r(a)
                if b is not None:
                    bonus_sum(b)
                if c is not None:
                    ffn_k(c)
                    ffn_r(c)
                if b is not None:
                    gather_half(b, 1)
                if c is not None:
                    ffn_v(c)

            pe.wait_ge(const_in, 16)
            pe.wait_ge(state_in, 48)
            pe.wait_ge(bonus_ready, 2)
            for a in range(HALVES):
                for r in range(2):
                    col = (a * 2 + r) * B
                    mm = nc.tensor.transpose(pc[0][:, col:col + B], state_rows[:, r, a * P:(a + 1) * P],
                                             ident[0:B, 0:B])
            mm.then_inc(state_tr_done, 1)
            round_(0, None, None, first=True)
            round_(1, 0, None)
            with pe.Fori(1, B - 1) as i:
                round_(i + 1, i, i - 1)
            round_(None, B - 1, B - 2)
            round_(None, None, B - 1)


PRE = "L0_xattn_"


def kernel(**inputs):
    import concourse.bacc as _bacc
    from concourse.bass_utils import run_bass_kernel_spmd as _run

    def get(name):
        return np.asarray(inputs[PRE + name])

    def halves(v):
        return v.reshape(HALVES, P).T

    def grouped(v):
        return v.reshape(H, Q, G).transpose(2, 0, 1).reshape(P, Q)

    def grouped_out(m):
        return m.reshape(H, Q, G, E).transpose(3, 1, 2, 0).reshape(E, E)

    maa = get("maa_stack").reshape(NMIX, E)
    cols = []
    for name in VECS:
        if name.startswith("gn_"):
            cols.append(grouped(get(name)))
        elif name[:3] == "maa" and name[3:].isdigit():
            cols.append(halves(maa[int(name[3:])]))
        else:
            cols.append(halves(get(name).reshape(E)))
    arrays = {
        "x": np.asarray(inputs["x"]),
        "state": np.asarray(inputs["ctx_2048"]),
        "vecs": np.stack(cols, axis=1),
        "consts": constants(),
        "w1": get("maa_w1"),
        "w2": get("maa_w2"),
        "td1": get("td_w1"),
        "td2": get("td_w2"),
        "Wk": get("Wk").T,
        "Wr": get("Wr").T,
        "Wv": grouped_out(get("Wv")),
        "Wg": grouped_out(get("Wg")),
        "Wo": get("Wo").reshape(E, H, Q, G).transpose(2, 3, 1, 0).reshape(E, E),
        "Wfk": get("Wfk").T,
        "Wfr": get("Wfr").T,
        "Wfv": get("Wfv").T,
    }
    arrays = {f"in_{n}": np.ascontiguousarray(a) for n, a in arrays.items()}
    nc = _bacc.Bacc("TRN2", target_bir_lowering=False, num_devices=1)
    d = {n[3:]: nc.dram_tensor(n, a.shape, mybir.dt.from_np(a.dtype), kind="ExternalInput").ap()
         for n, a in arrays.items()}
    out = nc.dram_tensor("out_0", (B, L, E), F32, kind="ExternalOutput").ap()
    rwkv_block(nc, d["x"], d["state"], d["vecs"], d["consts"], d["w1"], d["w2"], d["td1"], d["td2"],
               {m: d[m] for m in MATS}, out)
    r = _run(nc, [arrays], core_ids=[0])
    return r.results[0]["out_0"]
```

```python
from contextlib import ExitStack

import numpy as np

import concourse.bass as bass
from concourse import mybir

ALU = mybir.AluOpType
ACT = mybir.ActivationFunctionType
F32 = mybir.dt.float32
F32R = mybir.dt.float32r

B, L, E, H = 4, 256, 256, 32
S = E // H
P = 128
HALVES = E // P
TILES = L // P
G = P // H
Q = S // G
HH = P // S
DM, DD, NMIX = 32, 64, 5
MIX_W, MIX_K, MIX_V, MIX_R, MIX_G = 1, 0, 2, 3, 4
MIX_ORDER = (MIX_K, MIX_V, MIX_W, MIX_R, MIX_G)
MIX_BANK = (0, 1, 2, 0, 0)
CHUNKS = HALVES * G
TB = L // G
EPS = 1e-5
WARM_UP = 6
PAIRS = 3
HALF = P // 2

VECS = ["ln1_w", "ln1_b", "ln2_w", "ln2_b", "maa_x", "maa0", "maa1", "maa2", "maa3", "maa4",
        "time_decay", "u", "ffn_maa_k", "ffn_maa_r", "gn_w", "gn_b"]
MATS = ["Wk", "Wv", "Wr", "Wg", "Wo", "Wfk", "Wfr", "Wfv"]


def constants():
    p, m = np.arange(P)[:, None], np.arange(P)[None, :]
    ident = (p == m)
    spread = [p == H * g + HH * half + m // S for half in range(HALVES) for g in range(G)]
    gather = [np.arange(H)[None, :] == HH * half + p // S for half in range(HALVES)]
    mean = (p % H == m % H) / S
    unblock = [p == H * tb + m % H for tb in range(G)]
    lower, odd = p >= HALF, p // DM % 2 == 1
    early = np.concatenate([ident, *gather, mean, mean[:, 0:H], lower, odd], axis=1).astype(np.float32)
    late = np.concatenate([*spread, *unblock], axis=1).astype(np.float32)
    return early, late


def rwkv_block(nc, x, state, vecs, early, late, w1, w2, td1, td2, mats, out):
    with ExitStack() as ctx:
        def sb(name, shape, dt=F32):
            return ctx.enter_context(nc.sbuf_tensor(name, shape, dt))

        def bank(name):
            return ctx.enter_context(nc.psum_tensor(name, [P, HALVES * L], F32))

        def sem(name):
            return ctx.enter_context(nc.semaphore(name))

        vec_sb = sb("vec_sb", [P, len(VECS), HALVES])
        early_sb = sb("early_sb", [P, early.shape[1]])
        ident = early_sb[:, 0:P]
        gather = early_sb[:, P:P + HALVES * H].rearrange("p (a h) -> p a h", h=H)
        mean_at = P + HALVES * H
        head_mean = early_sb[:, mean_at:mean_at + P]
        head_mean_row = early_sb[:, mean_at + P:mean_at + P + H]
        lower_rows, odd_blocks = early_sb[:, mean_at + P + H:mean_at + P + H + 1], early_sb[:, mean_at + P + H + 1:]
        late_sb = sb("late_sb", [P, late.shape[1]])
        spread = late_sb[:, 0:CHUNKS * P].rearrange("p (c m) -> p c m", m=P)
        unblock = late_sb[:, CHUNKS * P:].rearrange("p (b m) -> p b m", m=P)
        spread_r = sb("spread_r", [P, CHUNKS, P], F32R)
        bonus = sb("bonus", [P, HALVES, G, H])
        w1_sb = sb("w1_sb", [P, HALVES, PAIRS, P])
        w2_sb = sb("w2_sb", [P, NMIX, E])
        w2_hi = sb("w2_hi", [P, NMIX, E], F32R)
        w2_lo = sb("w2_lo", [P, NMIX - 1, E], F32R)
        w2_odd = sb("w2_odd", [P, E], F32R)
        td1_sb = sb("td1_sb", [P, HALVES, P])
        td2_sb = sb("td2_sb", [P, E])
        td2_hi = sb("td2_hi", [P, E], F32R)
        td2_lo = sb("td2_lo", [P, E], F32R)
        blank = sb("blank", [P, L])
        W = {m: sb(f"{m}_sb", [P, HALVES, E]) for m in MATS}
        state_rows = sb("state_rows", [B, 2, E])
        s0 = sb("s0", [P, HALVES, B, S])
        eps = sb("eps", [P, 1])

        x_sb = sb("x_sb", [P, B, TILES, E])
        xc = sb("xc", [P, B, HALVES, L + 1])
        k_sb = sb("k_sb", [P, B, HALVES, L])
        v_sb = sb("v_sb", [P, B, Q, L])
        g_sb = sb("g_sb", [P, B, Q, L])
        decay = sb("decay", [P, B, HALVES, Q, L])
        y_sb = sb("y_sb", [P, B, TILES, E])

        stats1 = sb("stats1", [P, B * TILES, 6])
        mv1 = sb("mv1", [P, B * TILES, 2])
        std1 = sb("std1", [P, B * TILES])
        rstd1 = sb("rstd1", [P, B * TILES])
        shift_1 = sb("shift_1", [P, B * TILES])
        xn = sb("xn", [P, TILES, E])
        xa = sb("xa", [P, HALVES, L + 1])
        before = sb("before", [P, B, HALVES])
        r_sb = sb("r_sb", [P, HALVES, L])
        sx = sb("sx", [P, HALVES, L])
        xin = sb("xin", [P, HALVES, L])
        lora = sb("lora", [P, PAIRS, L])
        lora_hi = sb("lora_hi", [P, PAIRS, L], F32R)
        lora_hl = sb("lora_hl", [P, PAIRS, L], F32R)
        td_hid = sb("td_hid", [P, L])
        td_hi = sb("td_hi", [P, L], F32R)
        td_hl = sb("td_hl", [P, L], F32R)
        xm = [sb(f"xm{j}", [P, HALVES, L]) for j in range(NMIX)]
        v_hi = sb("v_hi", [P, Q, L], F32R)
        v_lo = sb("v_lo", [P, Q, L], F32R)
        th_g = sb("th_g", [P, Q, L])
        ed = sb("ed", [P, HALVES, L])

        rec = sb("rec", [P, CHUNKS, Q, L])
        rk = sb("rk", [P, HALVES, L])
        vr = sb("vr", [P, Q, L])
        o_sb = sb("o_sb", [P, Q, L])
        cen = sb("cen", [P, Q, L])
        sq = sb("sq", [P, Q, L])
        std_o = sb("std_o", [P, TB])
        rstd_o = sb("rstd_o", [P, TB])
        on = sb("on", [P, Q, L])
        gated = sb("gated", [P, Q, L])

        x1 = sb("x1", [P, TILES, E])
        stats2 = sb("stats2", [P, TILES, 6])
        mdiff2, within2, msum2, between2 = (sb(n, [P, TILES]) for n in ("mdiff2", "within2", "msum2", "between2"))
        mv2 = sb("mv2", [P, TILES, 2])
        unused = sb("unused", [P, 1])
        std2 = sb("std2", [P, TILES])
        rstd2 = sb("rstd2", [P, TILES])
        xn2 = sb("xn2", [P, TILES, E])
        sx2 = sb("sx2", [P, HALVES, L])
        xk2 = sb("xk2", [P, HALVES, L])
        xr2 = sb("xr2", [P, HALVES, L])
        relu = sb("relu", [P, HALVES, L])
        kk = sb("kk", [P, HALVES, L])
        th_r = sb("th_r", [P, TILES, E])
        f1 = sb("f1", [P, TILES, E])

        pa = [bank(f"pa{i}") for i in range(3)]
        pv = [bank(f"pv{i}") for i in range(2)]
        py = bank("py")
        pc = [bank(f"pc{i}") for i in range(2)]

        def last(b):
            return isinstance(b, int) and b == B - 1

        def banks(b):
            return pa[0:2] if last(b) else pc

        def value_banks(b):
            return pv if last(b) else pc

        def by2(b):
            return b[:].rearrange("p (a t) -> p a t", a=2)

        def vcol(name, a):
            return vec_sb[:, VECS.index(name), a:a + 1]

        x_in, vec_in, early_in, late_in, state_in, s0_in = (sem(n) for n in (
            "x_in", "vec_in", "early_in", "late_in", "state_in", "s0_in"))
        x_rest_in = sem("x_rest_in")
        w2_hi_ready, w2_lo_ready, td2_hi_ready, td2_lo_ready = (sem(n) for n in (
            "w2_hi_ready", "w2_lo_ready", "td2_hi_ready", "td2_lo_ready"))
        w1_in, w2_in, td_in, out_done = (sem(n) for n in ("w1_in", "w2_in", "td_in", "out_done"))
        mat_in = {m: sem(f"{m}_in") for m in MATS}
        zeroed, stats1_ready, mv1_ready, std1_ready, rstd1_ready = (sem(n) for n in (
            "zeroed", "stats1_ready", "mv1_ready", "std1_ready", "rstd1_ready"))
        state_tr_done, state_cols_ready, bonus_ready, spread_ready = (sem(n) for n in (
            "state_tr_done", "state_cols_ready", "bonus_ready", "spread_ready"))
        xn_ready, sx_ready, xin_ready, m_ready, g_ready = (sem(n) for n in (
            "xn_ready", "sx_ready", "xin_ready", "m_ready", "g_ready"))
        a_ready, scan_done, vr_ready, o_ready, cen_ready, rstdo_ready = (sem(n) for n in (
            "a_ready", "scan_done", "vr_ready", "o_ready", "cen_ready", "rstdo_ready"))
        on_ready, gated_ready, x1_ready, stats2_ready, mv2_ready, rstd2_ready = (sem(n) for n in (
            "on_ready", "gated_ready", "x1_ready", "stats2_ready", "mv2_ready", "rstd2_ready"))
        xn2_ready, xk2_ready, xr2_ready, f1_ready, y_ready = (sem(n) for n in (
            "xn2_ready", "xk2_ready", "xr2_ready", "f1_ready", "y_ready"))
        mdiff_ready, between_ready = sem("mdiff_ready"), sem("between_ready")
        xa_ready, lora_ready, tdh_ready, k_ready, v_ready, r_ready, thg_ready, ed_ready, w_ready = (sem(n) for n in (
            "xa_ready", "lora_ready", "tdh_ready", "k_ready", "v_ready", "r_ready", "thg_ready", "ed_ready",
            "w_ready"))
        lora_hi_ready, tdh_hi_ready = sem("lora_hi_ready"), sem("tdh_hi_ready")
        lora_lo_ready, tdh_lo_ready = sem("lora_lo_ready"), sem("tdh_lo_ready")
        sq_ready, stdo_ready, std2_ready, xc_ready, relu_ready, kk_ready, thr_ready = (sem(n) for n in (
            "sq_ready", "stdo_ready", "std2_ready", "xc_ready", "relu_ready", "kk_ready", "thr_ready"))
        xm_ready, s0_placed, p_ready, rk_ready, sx2_ready = (sem(n) for n in (
            "xm_ready", "s0_placed", "p_ready", "rk_ready", "sx2_ready"))
        vlo_ready, vhi_ready = sem("vlo_ready"), sem("vhi_ready")
        tr1_done, w1_done, w2_done, td1_done, td2_done, pk_done, pvv_done, pr_done, pg_done = (sem(n) for n in (
            "tr1_done", "w1_done", "w2_done", "td1_done", "td2_done", "pk_done", "pvv_done", "pr_done",
            "pg_done"))
        spread_done, gather_done, bonus_done, mean_done, var_done, unblock_done = (sem(n) for n in (
            "spread_done", "gather_done", "bonus_done", "mean_done", "var_done", "unblock_done"))
        wo_done, tr2_done, fk_done, fr_done, fv_done = (sem(n) for n in (
            "wo_done", "tr2_done", "fk_done", "fr_done", "fv_done"))

        block = ctx.enter_context(nc.Block())

        @block.sync
        def _(sp):
            x_tiles = x.rearrange("b (t p) e -> p b t e", p=P)
            sp.dma_start(x_sb[:, 0], x_tiles[:, 0]).then_inc(x_in, 16)
            sp.dma_start(early_sb[:], early).then_inc(early_in, 16)
            sp.dma_start(vec_sb[:], vecs).then_inc(vec_in, 16)
            sp.dma_start(state_rows[:], state[:, 0:2, :]).then_inc(state_in, 16)
            sp.dma_start(w1_sb[:], w1.rearrange("(a p) (c m) -> p a c m", p=P, m=P)).then_inc(w1_in, 16)
            sp.dma_start(w2_sb[:], w2).then_inc(w2_in, 16)
            sp.dma_start(td1_sb[:], td1.rearrange("(a p) n -> p a n", p=P)).then_inc(td_in, 16)
            sp.dma_start(td2_sb[:], td2).then_inc(td_in, 16)
            sp.dma_start(W["Wk"][:], mats["Wk"].rearrange("(a p) n -> p a n", p=P)).then_inc(mat_in["Wk"], 16)
            sp.dma_start(x_sb[:, 1:B], x_tiles[:, 1:B]).then_inc(x_rest_in, 16)
            for m in ("Wv", "Wg", "Wr"):
                sp.dma_start(W[m][:], mats[m].rearrange("(a p) n -> p a n", p=P)).then_inc(mat_in[m], 16)
            s0_rows = state.rearrange("b r e -> b (r e)")[:, 2 * E:(2 + S) * E]
            for a in range(HALVES):
                half = s0_rows[:, a * P * S:(a + 1) * P * S]
                sp.dma_start(s0[:, a], half.rearrange("b (p j) -> p b j", j=S)).then_inc(s0_in, 16)
            sp.dma_start(late_sb[:], late).then_inc(late_in, 16)
            for m in ("Wo", "Wfk", "Wfr", "Wfv"):
                sp.dma_start(W[m][:], mats[m].rearrange("(a p) n -> p a n", p=P)).then_inc(mat_in[m], 16)
            with sp.Fori(0, B - 1) as b:
                sp.wait_ge(y_ready, TILES * b + TILES)
                sp.dma_start(out[b].rearrange("(t p) e -> p t e", p=P), y_sb[:, b]).then_inc(out_done, 16)
            for t in range(TILES):
                sp.wait_ge(y_ready, TILES * (B - 1) + t + 1)
                sp.dma_start(out[B - 1, t * P:(t + 1) * P, :], y_sb[:, B - 1, t]).then_inc(out_done, 16)
            sp.wait_ge(out_done, 16 * (B - 1 + TILES))

        @block.gpsimd
        def _(pool):
            def s0_place(b):
                if isinstance(b, int) and b == 0:
                    pool.wait_ge(s0_in, 16 * HALVES)
                else:
                    pool.wait_ge(gather_done, 2 * b)
                for a in range(HALVES):
                    dst = rec[:, G * a:G * a + G, :, 0]
                    src = s0[:, a, b, :].rearrange("p (q g) -> p g q", g=G)
                    nc.gpsimd.tensor_copy(dst, src).then_inc(s0_placed, 1)

            def product(b, c):
                if c == 0:
                    pool.wait_ge(r_ready, b + 1)
                pool.wait_ge(scan_done, CHUNKS * b + c + 1)
                r_b = r_sb[:, c // G, :].unsqueeze(1).broadcast_to([P, Q, L])
                nc.gpsimd.tensor_tensor(rec[:, c], rec[:, c], r_b, ALU.mult).then_inc(p_ready, 1)

            def mixed(n, i):
                j = MIX_ORDER[i]
                pool.wait_ge(m_ready, 10 * n + 2 * i + 2)
                nc.gpsimd.tensor_tensor(xm[j][:], xm[j][:], xa[:, :, 1:L + 1], ALU.add).then_inc(xm_ready, 1)

            def rk_product(b):
                pool.wait_ge(k_ready, b + 1)
                pool.wait_ge(r_ready, b + 1)
                if not isinstance(b, int) or b:
                    pool.wait_ge(bonus_done, b)
                nc.gpsimd.tensor_tensor(rk[:], r_sb[:], k_sb[:, b], ALU.mult).then_inc(rk_ready, 1)

            def shift2(b, a):
                pool.wait_ge(xc_ready, 2 * b + a + 1)
                nc.gpsimd.tensor_tensor(sx2[:, a], xc[:, b, a, 0:L], xc[:, b, a, 1:L + 1],
                                        ALU.subtract).then_inc(sx2_ready, 1)

            def v_low(n):
                pool.wait_ge(vhi_ready, n + 1)
                pool.wait_ge(v_ready, n + 1)
                nc.gpsimd.tensor_tensor(v_lo[:], v_sb[:, n], v_hi[:].bitcast(F32), ALU.subtract).then_inc(vlo_ready, 1)

            def lora_low(n, c):
                pool.wait_ge(lora_hi_ready, PAIRS * n + c + 1)
                nc.gpsimd.tensor_tensor(lora_hl[:, c], lora[:, c], lora_hi[:, c].bitcast(F32),
                                        ALU.subtract).then_inc(lora_lo_ready, 1)

            def td_low(n):
                pool.wait_ge(tdh_hi_ready, n + 1)
                nc.gpsimd.tensor_tensor(td_hl[:], td_hid[:], td_hi[:].bitcast(F32),
                                        ALU.subtract).then_inc(tdh_lo_ready, 1)

            def split_low(i):
                j = MIX_ORDER[i]
                if j == MIX_G:
                    pool.wait_ge(w2_hi_ready, 3)
                    nc.gpsimd.tensor_tensor(w2_hi[:, j], w2_sb[:, j], w2_odd[:].bitcast(F32),
                                            ALU.subtract).then_inc(w2_lo_ready, 1)
                else:
                    pool.wait_ge(w2_hi_ready, j // 2 + 1)
                    nc.gpsimd.tensor_tensor(w2_lo[:, j], w2_sb[:, j], w2_hi[:, j].bitcast(F32),
                                            ALU.subtract).then_inc(w2_lo_ready, 1)

            def split_low_td():
                pool.wait_ge(td2_hi_ready, 1)
                nc.gpsimd.tensor_tensor(td2_lo[:], td2_sb[:], td2_hi[:].bitcast(F32),
                                        ALU.subtract).then_inc(td2_lo_ready, 1)

            nc.gpsimd.memset(eps[:], EPS).then_inc(zeroed, 1)
            nc.gpsimd.memset(blank[:], 0.0).then_inc(zeroed, 1)
            nc.gpsimd.memset(decay[:, :, :, :, 0], 0.0).then_inc(zeroed, 1)
            split_low(0)
            split_low(1)
            split_low(2)
            split_low(3)
            split_low_td()
            split_low(4)
            mixed(0, 0)
            mixed(0, 1)
            mixed(0, 2)
            mixed(0, 3)
            mixed(0, 4)
            s0_place(0)
            v_low(0)
            rk_product(0)
            product(0, 0)
            lora_low(1, 0)
            product(0, 1)
            lora_low(1, 1)
            lora_low(1, 2)
            product(0, 2)
            mixed(1, 0)
            mixed(1, 1)
            mixed(1, 2)
            product(0, 3)
            mixed(1, 3)
            mixed(1, 4)
            td_low(1)
            product(0, 4)
            product(0, 5)
            product(0, 6)
            product(0, 7)
            v_low(1)
            with pool.Fori(1, B - 1) as i:
                s0_place(i)
                rk_product(i)
                product(i, 0)
                product(i, 1)
                lora_low(i + 1, 0)
                lora_low(i + 1, 1)
                mixed(i + 1, 0)
                mixed(i + 1, 1)
                mixed(i + 1, 2)
                product(i, 2)
                lora_low(i + 1, 2)
                product(i, 3)
                td_low(i + 1)
                shift2(i - 1, 0)
                shift2(i - 1, 1)
                mixed(i + 1, 3)
                mixed(i + 1, 4)
                product(i, 4)
                product(i, 5)
                product(i, 6)
                product(i, 7)
                v_low(i + 1)
            s0_place(B - 1)
            rk_product(B - 1)
            product(B - 1, 0)
            product(B - 1, 1)
            product(B - 1, 2)
            product(B - 1, 3)
            product(B - 1, 4)
            product(B - 1, 5)
            product(B - 1, 6)
            product(B - 1, 7)
            shift2(B - 2, 0)
            shift2(B - 2, 1)
        @block.scalar
        def _(act):
            def normalise1(n):
                if not isinstance(n, int) or n:
                    act.wait_ge(tr1_done, n)
                for t in range(TILES):
                    i = bass.ds(n * TILES + t, 1)
                    nc.scalar.activation(xn[:, t, :], x_sb[:, n, t, :], ACT.Identity, bias=shift_1[:, i],
                                         scale=rstd1[:, i]).then_inc(xn_ready, 1)

            def norm1(n, a):
                if a == 0:
                    act.wait_ge(tr1_done, n + 1)
                    if not isinstance(n, int) or n:
                        act.wait_ge(xm_ready, NMIX * n)
                    nc.scalar.activation(xa[:, :, 0], before[:, n, :], ACT.Copy).then_inc(xa_ready, 1)
                nc.scalar.activation(xa[:, a, 1:L + 1], pa[0][:, a * L:(a + 1) * L], ACT.Identity,
                                     bias=vcol("ln1_b", a), scale=vcol("ln1_w", a)).then_inc(xa_ready, 1)

            def lora_tanh(n, c):
                if not isinstance(n, int) or n:
                    act.wait_ge(lora_lo_ready, PAIRS * n)
                    act.wait_ge(w2_done, 5 * n)
                act.wait_ge(w1_done, PAIRS * n + c + 1)
                src = (pa[1][:, 0:L], pa[2][:, 0:L], pa[1][:, L:2 * L])[c]
                nc.scalar.activation(lora[:, c], src, ACT.Tanh).then_inc(lora_ready, 1)
                act.wait_ge(lora_ready, PAIRS * n + c + 1)
                nc.scalar.activation(lora_hi[:, c], lora[:, c], ACT.Identity,
                                     scale=lower_rows).then_inc(lora_hi_ready, 1)

            def td_tanh(n):
                if not isinstance(n, int) or n:
                    act.wait_ge(td2_done, n)
                act.wait_ge(td1_done, n + 1)
                nc.scalar.activation(td_hid[:], pa[2][:, 0:L], ACT.Tanh).then_inc(tdh_ready, 1)
                act.wait_ge(tdh_ready, n + 1)
                nc.scalar.activation(td_hi[:], td_hid[:], ACT.Identity, scale=lower_rows).then_inc(tdh_hi_ready, 1)

            def take_k(n):
                act.wait_ge(pk_done, n + 1)
                nc.scalar.activation(k_sb[:, n], by2(pa[1]), ACT.Copy).then_inc(k_ready, 1)

            def take_v(n):
                act.wait_ge(pvv_done, n + 1)
                if not isinstance(n, int) or n:
                    act.wait_ge(spread_done, CHUNKS * n)
                nc.scalar.activation(v_hi[:], by2(pa[1]), ACT.Copy).then_inc(vhi_ready, 1)
                nc.scalar.activation(v_sb[:, n], by2(pa[1]), ACT.Copy).then_inc(v_ready, 1)

            def take_r(n):
                act.wait_ge(pr_done, n + 1)
                if not isinstance(n, int) or n:
                    act.wait_ge(p_ready, CHUNKS * n)
                nc.scalar.activation(r_sb[:], by2(pa[2]), ACT.Copy).then_inc(r_ready, 1)

            def decays(n):
                act.wait_ge(td2_done, n + 1)
                if not isinstance(n, int) or n:
                    act.wait_ge(w_ready, 2 * n)
                for a in range(HALVES):
                    nc.scalar.activation(ed[:, a, :], pa[2][:, a * L:(a + 1) * L], ACT.Exp,
                                         bias=vcol("time_decay", a)).then_inc(ed_ready, 1)
                act.wait_ge(ed_ready, 2 * n + 2)
                for q in range(Q):
                    nc.scalar.activation(decay[:, n, :, q, 1:L], ed[:, :, 0:L - 1], ACT.Exp,
                                         scale=-1.0).then_inc(w_ready, 1)

            def gate_tanh(n):
                act.wait_ge(pg_done, n + 1)
                nc.scalar.activation(th_g[:], by2(pa[0]), ACT.Tanh, scale=0.5).then_inc(thg_ready, 1)

            def squares(b):
                act.wait_ge(cen_ready, b + 1)
                nc.scalar.activation(sq[:], cen[:], ACT.Square).then_inc(sq_ready, 1)

            def head_std(b):
                act.wait_ge(var_done, b + 1)
                nc.scalar.activation(std_o[:], banks(b)[0][:, 0:TB], ACT.Sqrt, bias=eps[:]).then_inc(stdo_ready, 1)

            def token_std(b):
                act.wait_ge(mv2_ready, 2 * b + 2)
                nc.scalar.activation(std2[:], mv2[:, :, 1], ACT.Sqrt, bias=eps[:],
                                     scale=1.0 if isinstance(b, int) else 1.0 / E).then_inc(std2_ready, 1)

            def norm2(b, a):
                act.wait_ge(tr2_done, 2 * b + a + 1)
                nc.scalar.activation(xc[:, b, a, 1:L + 1], banks(b)[a][:, 0:L], ACT.Identity, bias=vcol("ln2_b", a),
                                     scale=vcol("ln2_w", a)).then_inc(xc_ready, 1)

            def relu_squared(b, o):
                act.wait_ge(fk_done, 2 * b + o + 1)
                nc.scalar.activation(relu[:, o], banks(b)[o][:, 0:L], ACT.Relu).then_inc(relu_ready, 1)
                act.wait_ge(relu_ready, 2 * b + o + 1)
                nc.scalar.activation(kk[:, o], relu[:, o], ACT.Square).then_inc(kk_ready, 1)

            def receptance_tanh(b, t):
                act.wait_ge(fr_done, 2 * b + t + 1)
                nc.scalar.activation(th_r[:, t], pc[t][:, 0:E], ACT.Tanh, scale=0.5).then_inc(thr_ready, 1)

            def load_table(func):
                nc.scalar.activation(unused[:], eps[:], func)

            def split_high(part):
                if part == 0:
                    act.wait_ge(w2_in, 16)
                    nc.scalar.activation(w2_hi[:, 0:2], w2_sb[:, 0:2], ACT.Copy).then_inc(w2_hi_ready, 1)
                elif part == 1:
                    nc.scalar.activation(w2_hi[:, 2:MIX_G], w2_sb[:, 2:MIX_G], ACT.Copy).then_inc(w2_hi_ready, 1)
                    act.wait_ge(early_in, 16)
                    nc.scalar.activation(w2_odd[:], w2_sb[:, MIX_G], ACT.Identity,
                                         scale=odd_blocks).then_inc(w2_hi_ready, 1)
                else:
                    act.wait_ge(td_in, 32)
                    nc.scalar.activation(td2_hi[:], td2_sb[:], ACT.Copy).then_inc(td2_hi_ready, 1)

            def std_1(first, end):
                act.wait_ge(mv1_ready, end)
                nc.scalar.activation(std1[:, first:end], mv1[:, first:end, 1], ACT.Sqrt,
                                     bias=eps[:]).then_inc(std1_ready, 1)

            act.wait_ge(zeroed, 3)
            load_table(ACT.Sqrt)
            std_1(0, TILES)
            act.wait_ge(rstd1_ready, 2)
            normalise1(0)
            act.wait_ge(state_tr_done, 1)
            rows = pc[0][:, 0:2 * 2 * B].rearrange("p (a r b) -> p b a r", a=HALVES, r=2)
            nc.scalar.activation(before[:], rows[:, :, :, 1], ACT.Copy).then_inc(state_cols_ready, 1)
            nc.scalar.activation(xc[:, :, :, 0], rows[:, :, :, 0], ACT.Copy).then_inc(state_cols_ready, 1)
            act.wait_ge(vec_in, 16)
            act.wait_ge(state_cols_ready, 1)
            norm1(0, 0)
            norm1(0, 1)
            split_high(0)
            split_high(2)
            split_high(1)
            lora_tanh(0, 0)
            lora_tanh(0, 1)
            lora_tanh(0, 2)
            std_1(TILES, B * TILES)
            take_k(0)
            td_tanh(0)
            act.wait_ge(rstd1_ready, 4)
            normalise1(1)
            take_v(0)
            gate_tanh(0)
            decays(0)
            norm1(1, 0)
            norm1(1, 1)
            take_r(0)
            lora_tanh(1, 0)
            lora_tanh(1, 1)
            lora_tanh(1, 2)
            take_k(1)
            td_tanh(1)
            take_v(1)
            decays(1)
            gate_tanh(1)
            take_r(1)
            with act.Fori(1, B - 1) as i:
                normalise1(i + 1)
                norm1(i + 1, 0)
                norm1(i + 1, 1)
                squares(i - 1)
                head_std(i - 1)
                lora_tanh(i + 1, 0)
                lora_tanh(i + 1, 1)
                lora_tanh(i + 1, 2)
                take_k(i + 1)
                token_std(i - 1)
                td_tanh(i + 1)
                norm2(i - 1, 0)
                norm2(i - 1, 1)
                decays(i + 1)
                relu_squared(i - 1, 0)
                relu_squared(i - 1, 1)
                receptance_tanh(i - 1, 0)
                take_v(i + 1)
                gate_tanh(i + 1)
                receptance_tanh(i - 1, 1)
                take_r(i + 1)
            squares(B - 2)
            head_std(B - 2)
            token_std(B - 2)
            norm2(B - 2, 0)
            load_table(ACT.Sqrt)
            norm2(B - 2, 1)
            squares(B - 1)
            relu_squared(B - 2, 0)
            head_std(B - 1)
            relu_squared(B - 2, 1)
            receptance_tanh(B - 2, 0)
            receptance_tanh(B - 2, 1)
            token_std(B - 1)
            load_table(ACT.Tanh)
            norm2(B - 1, 0)
            norm2(B - 1, 1)
            relu_squared(B - 1, 0)
            relu_squared(B - 1, 1)
            receptance_tanh(B - 1, 0)
            receptance_tanh(B - 1, 1)

        @block.vector
        def _(dve):
            def shift1(n, a):
                dve.wait_ge(xa_ready, 3 * n + 2 + a)
                nc.vector.tensor_tensor(sx[:, a], xa[:, a, 0:L], xa[:, a, 1:L + 1],
                                        ALU.subtract).then_inc(sx_ready, 1)
                dve.wait_ge(sx_ready, 2 * n + a + 1)
                nc.vector.scalar_tensor_tensor(xin[:, a, :], sx[:, a, :], vcol("maa_x", a), xa[:, a, 1:L + 1],
                                               ALU.mult, ALU.add).then_inc(xin_ready, 1)

            def lora_low(n, c):
                dve.wait_ge(lora_hi_ready, PAIRS * n + c + 1)
                nc.vector.tensor_tensor(lora_hl[:, c], lora[:, c], lora_hi[:, c].bitcast(F32),
                                        ALU.subtract).then_inc(lora_lo_ready, 1)

            def td_low(n):
                dve.wait_ge(tdh_hi_ready, n + 1)
                nc.vector.tensor_tensor(td_hl[:], td_hid[:], td_hi[:].bitcast(F32),
                                        ALU.subtract).then_inc(tdh_lo_ready, 1)

            def mix(n, i):
                j = MIX_ORDER[i]
                src = pa[MIX_BANK[i]]
                dve.wait_ge(w2_done, 5 * n + i + 1)
                for a in range(HALVES):
                    nc.vector.scalar_tensor_tensor(xm[j][:, a, :], src[:, a * L:(a + 1) * L], vcol(f"maa{j}", a),
                                                   sx[:, a, :], ALU.add, ALU.mult).then_inc(m_ready, 1)

            def gate(n):
                dve.wait_ge(thg_ready, n + 1)
                nc.vector.scalar_tensor_tensor(g_sb[:, n], th_g[:], 1.0, by2(pa[0]), ALU.add,
                                               ALU.mult).then_inc(g_ready, 1)

            def kv(b, c):
                if c == 0:
                    dve.wait_ge(k_ready, b + 1)
                    dve.wait_ge(s0_placed, 2 * b + 2)
                dve.wait_ge(spread_done, CHUNKS * b + c + 1)
                k_b = k_sb[:, b, c // G, 0:L - 1].unsqueeze(1).broadcast_to([P, Q, L - 1])
                nc.vector.tensor_tensor(rec[:, c, :, 1:L], by2(pv[c % 2])[:, :, 0:L - 1], k_b,
                                        ALU.mult).then_inc(a_ready, 1)

            def scan(b, c):
                if c == 0:
                    dve.wait_ge(w_ready, 2 * b + 2)
                dve.wait_ge(a_ready, CHUNKS * b + c + 1)
                rows = rec[:, c].rearrange("p q t -> p (q t)")
                nc.vector.tensor_tensor_scan(rows, decay[:, b, c // G].rearrange("p q t -> p (q t)"), rows, 0.0,
                                             ALU.mult, ALU.add).then_inc(scan_done, 1)

            def bonus_out(b):
                dve.wait_ge(bonus_done, b + 1)
                rb = pv[0][:, 0:L].unsqueeze(1).broadcast_to([P, Q, L])
                nc.vector.tensor_tensor(vr[:], rb, v_sb[:, b], ALU.mult).then_inc(vr_ready, 1)

            def wkv_out(b):
                dve.wait_ge(gather_done, 2 * b + 2)
                dve.wait_ge(vr_ready, b + 1)
                nc.vector.tensor_tensor(o_sb[:], by2(py), vr[:], ALU.add).then_inc(o_ready, 1)

            def centre(b):
                dve.wait_ge(mean_done, b + 1)
                mean = banks(b)[1][:, 0:L].unsqueeze(1).broadcast_to([P, Q, L])
                nc.vector.tensor_tensor(cen[:], o_sb[:], mean, ALU.subtract).then_inc(cen_ready, 1)

            def head_rstd(b):
                dve.wait_ge(stdo_ready, b + 1)
                nc.vector.reciprocal(rstd_o[:], std_o[:]).then_inc(rstdo_ready, 1)

            def gated_norm(b):
                dve.wait_ge(unblock_done, b + 1)
                for q in range(Q):
                    nc.vector.scalar_tensor_tensor(on[:, q, :], cen[:, q, :], vcol("gn_w", q), banks(b)[1][:, 0:L],
                                                   ALU.mult, ALU.mult).then_inc(on_ready, 1)
                dve.wait_ge(on_ready, 2 * b + 2)
                for q in range(Q):
                    nc.vector.scalar_tensor_tensor(gated[:, q, :], on[:, q, :], vcol("gn_b", q), g_sb[:, b, q, :],
                                                   ALU.add, ALU.mult).then_inc(gated_ready, 1)

            def residual(b, t):
                dve.wait_ge(wo_done, 2 * b + t + 1)
                nc.vector.scalar_tensor_tensor(x1[:, t], banks(b)[t][:, 0:E], 0.5, x_sb[:, b, t], ALU.mult,
                                               ALU.add).then_inc(x1_ready, 1)
                dve.wait_ge(x1_ready, 2 * b + t + 1)
                nc.vector.bn_stats(stats2[:, t, :], x1[:, t, :]).then_inc(stats2_ready, 1)

            def moments(b):
                if isinstance(b, int):
                    dve.wait_ge(stats2_ready, 2 * b + 2)
                    for t in range(TILES):
                        nc.vector.bn_aggr(mv2[:, t, :], stats2[:, t, :]).then_inc(mv2_ready, 1)
                    return
                even, odd = stats2[:, :, 1], stats2[:, :, 4]
                dve.wait_ge(stats2_ready, 2 * b + 2)
                nc.vector.tensor_tensor(mdiff2[:], even, odd, ALU.subtract).then_inc(mdiff_ready, 1)
                nc.vector.tensor_tensor(within2[:], stats2[:, :, 2], stats2[:, :, 5], ALU.add).then_inc(mdiff_ready, 1)
                nc.vector.tensor_tensor(msum2[:], even, odd, ALU.add).then_inc(mdiff_ready, 1)
                dve.wait_ge(mdiff_ready, 3 * b + 3)
                nc.vector.tensor_tensor(between2[:], mdiff2[:], mdiff2[:], ALU.mult).then_inc(between_ready, 1)
                nc.vector.tensor_scalar(mv2[:, :, 0], msum2[:], 0.5, None, ALU.mult).then_inc(mv2_ready, 1)
                dve.wait_ge(between_ready, b + 1)
                nc.vector.scalar_tensor_tensor(mv2[:, :, 1], between2[:], E / 4, within2[:], ALU.mult,
                                               ALU.add).then_inc(mv2_ready, 1)

            def normalise2(b):
                dve.wait_ge(std2_ready, b + 1)
                nc.vector.reciprocal(rstd2[:], std2[:]).then_inc(rstd2_ready, 1)
                dve.wait_ge(rstd2_ready, b + 1)
                for t in range(TILES):
                    nc.vector.tensor_scalar(xn2[:, t, :], x1[:, t, :], mv2[:, t, 0:1], rstd2[:, t:t + 1],
                                            ALU.subtract, ALU.mult).then_inc(xn2_ready, 1)

            def shift2(b, a):
                dve.wait_ge(xc_ready, 2 * b + a + 1)
                nc.vector.tensor_tensor(sx2[:, a], xc[:, b, a, 0:L], xc[:, b, a, 1:L + 1],
                                        ALU.subtract).then_inc(sx2_ready, 1)

            def mix2(b, name, a):
                dst, ready = (xk2, xk2_ready) if name == "ffn_maa_k" else (xr2, xr2_ready)
                dve.wait_ge(sx2_ready, 2 * b + a + 1)
                nc.vector.scalar_tensor_tensor(dst[:, a, :], sx2[:, a, :], vcol(name, a), xc[:, b, a, 1:L + 1],
                                               ALU.mult, ALU.add).then_inc(ready, 1)

            def finish(b, t):
                dve.wait_ge(thr_ready, 2 * b + t + 1)
                dve.wait_ge(fv_done, 2 * b + t + 1)
                nc.vector.scalar_tensor_tensor(f1[:, t], th_r[:, t], 1.0, value_banks(b)[t][:, 0:E], ALU.add,
                                               ALU.mult).then_inc(f1_ready, 1)
                dve.wait_ge(f1_ready, 2 * b + t + 1)
                nc.vector.scalar_tensor_tensor(y_sb[:, b, t], f1[:, t], 0.5, x1[:, t], ALU.mult,
                                               ALU.add).then_inc(y_ready, 1)

            def layer_norm_1(first, end):
                for i in range(first, end):
                    nc.vector.bn_stats(stats1[:, i, :], x_sb[:, i // TILES, i % TILES, :]).then_inc(stats1_ready, 1)
                for i in range(first, end):
                    dve.wait_ge(stats1_ready, i + 1)
                    nc.vector.bn_aggr(mv1[:, i, :], stats1[:, i, :]).then_inc(mv1_ready, 1)

            def scale_and_shift_1(first, end, part):
                dve.wait_ge(std1_ready, part)
                nc.vector.reciprocal(rstd1[:, first:end], std1[:, first:end]).then_inc(rstd1_ready, 1)
                dve.wait_ge(rstd1_ready, 2 * part - 1)
                nc.vector.scalar_tensor_tensor(shift_1[:, first:end], mv1[:, first:end, 0], -1.0,
                                               rstd1[:, first:end], ALU.mult, ALU.mult).then_inc(rstd1_ready, 1)

            def make_bonus():
                dve.wait_ge(early_in, 16)
                for a in range(HALVES):
                    g_b = gather[:, a, :].unsqueeze(1).broadcast_to([P, G, H])
                    nc.vector.tensor_scalar(bonus[:, a], g_b, vcol("u", a), None, ALU.mult).then_inc(bonus_ready, 1)

            def round_spreaders():
                dve.wait_ge(late_in, 16)
                nc.vector.tensor_copy(spread_r[:], spread).then_inc(spread_ready, 1)

            dve.wait_ge(x_in, 16)
            layer_norm_1(0, TILES)
            scale_and_shift_1(0, TILES, 1)
            dve.wait_ge(vec_in, 16)
            shift1(0, 0)
            shift1(0, 1)
            dve.wait_ge(x_rest_in, 16)
            layer_norm_1(1 * TILES, 2 * TILES)
            lora_low(0, 0)
            layer_norm_1(2 * TILES, 3 * TILES)
            lora_low(0, 1)
            mix(0, 0)
            lora_low(0, 2)
            mix(0, 1)
            mix(0, 2)
            mix(0, 3)
            layer_norm_1(3 * TILES, 4 * TILES)
            mix(0, 4)
            scale_and_shift_1(TILES, B * TILES, 2)
            round_spreaders()
            td_low(0)
            gate(0)
            kv(0, 0)
            scan(0, 0)
            shift1(1, 0)
            shift1(1, 1)
            kv(0, 1)
            kv(0, 2)
            scan(0, 1)
            scan(0, 2)
            kv(0, 3)
            mix(1, 0)
            scan(0, 3)
            mix(1, 1)
            mix(1, 2)
            kv(0, 4)
            kv(0, 5)
            mix(1, 3)
            scan(0, 4)
            scan(0, 5)
            kv(0, 6)
            mix(1, 4)
            scan(0, 6)
            kv(0, 7)
            make_bonus()
            scan(0, 7)
            bonus_out(0)
            gate(1)
            wkv_out(0)
            with dve.Fori(1, B - 1) as i:
                kv(i, 0)
                scan(i, 0)
                centre(i - 1)
                shift1(i + 1, 0)
                shift1(i + 1, 1)
                kv(i, 1)
                head_rstd(i - 1)
                scan(i, 1)
                kv(i, 2)
                kv(i, 3)
                gated_norm(i - 1)
                mix(i + 1, 0)
                mix(i + 1, 1)
                mix(i + 1, 2)
                kv(i, 4)
                scan(i, 2)
                residual(i - 1, 0)
                residual(i - 1, 1)
                moments(i - 1)
                scan(i, 3)
                normalise2(i - 1)
                mix(i + 1, 3)
                kv(i, 5)
                kv(i, 6)
                scan(i, 4)
                mix2(i - 1, "ffn_maa_k", 0)
                mix2(i - 1, "ffn_maa_k", 1)
                mix2(i - 1, "ffn_maa_r", 0)
                mix(i + 1, 4)
                mix2(i - 1, "ffn_maa_r", 1)
                scan(i, 5)
                kv(i, 7)
                scan(i, 6)
                scan(i, 7)
                bonus_out(i)
                gate(i + 1)
                finish(i - 1, 0)
                finish(i - 1, 1)
                wkv_out(i)
            kv(B - 1, 0)
            kv(B - 1, 1)
            scan(B - 1, 0)
            kv(B - 1, 2)
            centre(B - 2)
            scan(B - 1, 1)
            kv(B - 1, 3)
            scan(B - 1, 2)
            kv(B - 1, 4)
            head_rstd(B - 2)
            scan(B - 1, 3)
            kv(B - 1, 5)
            scan(B - 1, 4)
            gated_norm(B - 2)
            kv(B - 1, 6)
            scan(B - 1, 5)
            kv(B - 1, 7)
            scan(B - 1, 6)
            residual(B - 2, 0)
            scan(B - 1, 7)
            residual(B - 2, 1)
            moments(B - 2)
            normalise2(B - 2)
            bonus_out(B - 1)
            wkv_out(B - 1)
            mix2(B - 2, "ffn_maa_k", 0)
            mix2(B - 2, "ffn_maa_r", 0)
            mix2(B - 2, "ffn_maa_k", 1)
            centre(B - 1)
            mix2(B - 2, "ffn_maa_r", 1)
            head_rstd(B - 1)
            gated_norm(B - 1)
            finish(B - 2, 0)
            finish(B - 2, 1)
            residual(B - 1, 0)
            residual(B - 1, 1)
            moments(B - 1)
            normalise2(B - 1)
            shift2(B - 1, 0)
            mix2(B - 1, "ffn_maa_k", 0)
            shift2(B - 1, 1)
            mix2(B - 1, "ffn_maa_k", 1)
            mix2(B - 1, "ffn_maa_r", 0)
            mix2(B - 1, "ffn_maa_r", 1)
            finish(B - 1, 0)
            finish(B - 1, 1)

        @block.tensor
        def _(pe):
            def two_halves(dst, w, rhs, cols=HALVES):
                for o in range(cols):
                    for a in range(HALVES):
                        mm = nc.tensor.matmul(dst[:, o * L:(o + 1) * L], w[:, a, o * P:(o + 1) * P], rhs[:, a, :],
                                              start=(a == 0), stop=(a == HALVES - 1))
                return mm

            def tile_product(dst, act_t, w, t, a, done):
                mm = nc.tensor.matmul(dst[:, 0:E], act_t[:, a, t * P:(t + 1) * P], w[:, a, :], start=(a == 0),
                                      stop=(a == HALVES - 1))
                if a == HALVES - 1:
                    mm.then_inc(done, 1)

            def tr1(n):
                pe.wait_ge(xn_ready, 2 * n + 2)
                if not isinstance(n, int) or n:
                    pe.wait_ge(g_ready, n)
                for a in range(HALVES):
                    for t in range(TILES):
                        mm = nc.tensor.transpose(pa[0][:, a * L + t * P:a * L + (t + 1) * P],
                                                 xn[:, t, a * P:(a + 1) * P], ident)
                mm.then_inc(tr1_done, 1)

            def lora_in(n, step):
                if step == 0:
                    pe.wait_ge(xin_ready, 2 * n + 1)
                    if not isinstance(n, int) or n:
                        pe.wait_ge(v_ready, n)
                elif step == 1:
                    pe.wait_ge(xin_ready, 2 * n + 2)
                elif step == 2 and (not isinstance(n, int) or n):
                    pe.wait_ge(r_ready, n)
                elif step == 3:
                    pe.wait_ge(lora_ready, PAIRS * n + 1)
                c = max(step - 1, 0)
                dst = (pa[1][:, 0:L], pa[2][:, 0:L], pa[1][:, L:2 * L])[c]
                for a in {0: (0,), 1: (1,)}.get(step, range(HALVES)):
                    mm = nc.tensor.matmul(dst, w1_sb[:, a, c], xin[:, a, :], start=(a == 0), stop=(a == HALVES - 1))
                if step:
                    mm.then_inc(w1_done, 1)

            def lora_out(n, i):
                j = MIX_ORDER[i]
                pe.wait_ge(lora_lo_ready, PAIRS * n + j // 2 + 1)
                if i == 1:
                    pe.wait_ge(lora_ready, PAIRS * n + 3)
                elif i == 2:
                    pe.wait_ge(lora_ready, PAIRS * n + 2)
                elif i == 3:
                    pe.wait_ge(m_ready, 10 * n + 2)
                elif i == 4:
                    pe.wait_ge(m_ready, 10 * n + 8)
                weights = (w2_hi,) if j == NMIX - 1 else (w2_hi, w2_lo)
                for o in range(HALVES):
                    for w in weights:
                        mm = nc.tensor.matmul(pa[MIX_BANK[i]][:, o * L:(o + 1) * L], w[:, j, o * P:(o + 1) * P],
                                              lora_hl[:, j // 2, :], start=(w is weights[0]), stop=(w is weights[-1]))
                mm.then_inc(w2_done, 1)

            def td_in_(n):
                pe.wait_ge(xm_ready, 5 * n + 3)
                two_halves(pa[2], td1_sb, xm[MIX_W], cols=1).then_inc(td1_done, 1)

            def td_out(n):
                pe.wait_ge(tdh_lo_ready, n + 1)
                for o in range(HALVES):
                    for w in (td2_hi, td2_lo):
                        mm = nc.tensor.matmul(pa[2][:, o * L:(o + 1) * L], w[:, o * P:(o + 1) * P], td_hl[:],
                                              start=(w is td2_hi), stop=(w is td2_lo))
                mm.then_inc(td2_done, 1)

            def project_k(n):
                pe.wait_ge(m_ready, 10 * n + 4)
                pe.wait_ge(xm_ready, 5 * n + 1)
                two_halves(pa[1], W["Wk"], xm[MIX_K]).then_inc(pk_done, 1)

            def project_v(n):
                pe.wait_ge(k_ready, n + 1)
                pe.wait_ge(xm_ready, 5 * n + 2)
                two_halves(pa[1], W["Wv"], xm[MIX_V]).then_inc(pvv_done, 1)

            def project_r(n):
                pe.wait_ge(ed_ready, 2 * n + 2)
                pe.wait_ge(xm_ready, 5 * n + 4)
                two_halves(pa[2], W["Wr"], xm[MIX_R]).then_inc(pr_done, 1)

            def project_g(n):
                pe.wait_ge(xm_ready, 5 * n + 5)
                two_halves(pa[0], W["Wg"], xm[MIX_G]).then_inc(pg_done, 1)

            def spread_v(b, c):
                if c == 0:
                    pe.wait_ge(vlo_ready, b + 1)
                    if not isinstance(b, int) or b:
                        pe.wait_ge(vr_ready, b)
                elif c >= 2:
                    pe.wait_ge(a_ready, CHUNKS * b + c - 1)
                for part, v in enumerate((v_hi, v_lo)):
                    mm = nc.tensor.matmul(pv[c % 2][:], spread_r[:, c, :], v[:].rearrange("p q t -> p (q t)"),
                                          start=(part == 0), stop=(part == 1))
                mm.then_inc(spread_done, 1)

            def gather_half(b, a):
                pe.wait_ge(p_ready, CHUNKS * b + G * (a + 1))
                if a == 0 and (not isinstance(b, int) or b):
                    pe.wait_ge(o_ready, b)
                for g in range(G):
                    mm = nc.tensor.matmul(py[H * g:H * (g + 1), :], gather[:, a, :],
                                          rec[:, G * a + g].rearrange("p q t -> p (q t)"), start=(a == 0),
                                          stop=(a == HALVES - 1))
                mm.then_inc(gather_done, 1)

            def bonus_sum(b):
                pe.wait_ge(rk_ready, b + 1)
                pe.wait_ge(a_ready, CHUNKS * b + CHUNKS - 1)
                for a in range(HALVES):
                    mm = nc.tensor.matmul(pv[0][:, 0:L], bonus[:, a].rearrange("p g h -> p (g h)"), rk[:, a, :],
                                          start=(a == 0), stop=(a == HALVES - 1))
                mm.then_inc(bonus_done, 1)

            def head_sum(dst, src, done):
                for q in range(Q):
                    mm = nc.tensor.matmul(dst[:, 0:L], head_mean, src[:, q, :], start=(q == 0), stop=(q == Q - 1))
                mm.then_inc(done, 1)

            def mean_(b):
                pe.wait_ge(o_ready, b + 1)
                if not isinstance(b, int) or 0 < b < B - 1:
                    pe.wait_ge(f1_ready, 2 * b)
                head_sum(banks(b)[1], o_sb, mean_done)

            def var_(b):
                pe.wait_ge(sq_ready, b + 1)
                for q in range(Q):
                    for tb in range(G):
                        mm = nc.tensor.matmul(banks(b)[0][H * tb:H * (tb + 1), 0:TB], head_mean_row,
                                              sq[:, q, tb * TB:(tb + 1) * TB], start=(q == 0), stop=(q == Q - 1))
                mm.then_inc(var_done, 1)

            def unblock_rstd(b):
                pe.wait_ge(rstdo_ready, b + 1)
                for tb in range(G):
                    mm = nc.tensor.matmul(banks(b)[1][:, tb * TB:(tb + 1) * TB], unblock[:, tb, :], rstd_o[:],
                                          start=True, stop=True)
                mm.then_inc(unblock_done, 1)

            def out_product(b, a):
                pe.wait_ge(gated_ready, 2 * b + a + 1)
                for t in range(TILES):
                    tile_product(banks(b)[t], gated, W["Wo"], t, a, wo_done)

            def tr2(b):
                pe.wait_ge(xn2_ready, 2 * b + 2)
                for a in range(HALVES):
                    for t in range(TILES):
                        mm = nc.tensor.transpose(banks(b)[a][:, t * P:(t + 1) * P], xn2[:, t, a * P:(a + 1) * P], ident)
                    mm.then_inc(tr2_done, 1)

            def ffn_k(b, a):
                pe.wait_ge(xk2_ready, 2 * b + a + 1)
                if a == 0:
                    pe.wait_ge(xc_ready, 2 * b + 2)
                for o in range(HALVES):
                    mm = nc.tensor.matmul(banks(b)[o][:, 0:L], W["Wfk"][:, a, o * P:(o + 1) * P], xk2[:, a, :],
                                          start=(a == 0), stop=(a == HALVES - 1))
                    if a == HALVES - 1:
                        mm.then_inc(fk_done, 1)

            def ffn_r(b, t):
                pe.wait_ge(xr2_ready, 2 * b + 2)
                if last(b):
                    pe.wait_ge(f1_ready, 2 * b)
                else:
                    pe.wait_ge(relu_ready, 2 * b + t + 1)
                for a in range(HALVES):
                    tile_product(pc[t], xr2, W["Wfr"], t, a, fr_done)

            def ffn_v(b, t):
                pe.wait_ge(kk_ready, 2 * b + 2)
                if not last(b):
                    pe.wait_ge(thr_ready, 2 * b + t + 1)
                for a in range(HALVES):
                    tile_product(value_banks(b)[t], kk, W["Wfv"], t, a, fv_done)

            def keep_clock(idle_bank):
                nc.tensor.matmul(idle_bank[:, 0:L], ident, early_sb[:, 0:L], start=True, stop=True)

            pe.wait_ge(zeroed, 2)
            for _ in range(WARM_UP):
                nc.tensor.matmul(pa[2][:, 0:L], blank[:, 0:P], blank[:], start=True, stop=True)
            pe.wait_ge(early_in, 16)
            pe.wait_ge(state_in, 16)
            for a in range(HALVES):
                for r in range(2):
                    col = (a * 2 + r) * B
                    mm = nc.tensor.transpose(pc[0][:, col:col + B], state_rows[:, r, a * P:(a + 1) * P],
                                             ident[0:B, 0:B])
            mm.then_inc(state_tr_done, 1)
            tr1(0)
            keep_clock(pc[1])
            pe.wait_ge(w1_in, 16)
            lora_in(0, 0)
            lora_in(0, 1)
            lora_in(0, 2)
            lora_in(0, 3)
            pe.wait_ge(w2_lo_ready, 1)
            lora_out(0, 0)
            pe.wait_ge(w2_lo_ready, 2)
            lora_out(0, 1)
            pe.wait_ge(w2_lo_ready, 3)
            lora_out(0, 2)
            pe.wait_ge(w2_lo_ready, 4)
            lora_out(0, 3)
            pe.wait_ge(mat_in["Wk"], 16)
            project_k(0)
            pe.wait_ge(w2_lo_ready, 5)
            lora_out(0, 4)
            pe.wait_ge(td_in, 32)
            td_in_(0)
            pe.wait_ge(mat_in["Wv"], 16)
            project_v(0)
            pe.wait_ge(mat_in["Wg"], 16)
            project_g(0)
            pe.wait_ge(td2_lo_ready, 1)
            td_out(0)
            tr1(1)
            pe.wait_ge(spread_ready, 1)
            spread_v(0, 0)
            pe.wait_ge(mat_in["Wr"], 16)
            project_r(0)
            lora_in(1, 0)
            spread_v(0, 1)
            lora_in(1, 1)
            spread_v(0, 2)
            lora_in(1, 2)
            spread_v(0, 3)
            lora_in(1, 3)
            lora_out(1, 0)
            lora_out(1, 1)
            spread_v(0, 4)
            lora_out(1, 2)
            lora_out(1, 3)
            spread_v(0, 5)
            spread_v(0, 6)
            project_k(1)
            spread_v(0, 7)
            lora_out(1, 4)
            td_in_(1)
            gather_half(0, 0)
            project_v(1)
            td_out(1)
            pe.wait_ge(bonus_ready, 2)
            bonus_sum(0)
            project_g(1)
            project_r(1)
            gather_half(0, 1)
            pe.wait_ge(late_in, 16)
            for m in ("Wo", "Wfk", "Wfr", "Wfv"):
                pe.wait_ge(mat_in[m], 16)
            with pe.Fori(1, B - 1) as i:
                spread_v(i, 0)
                tr1(i + 1)
                mean_(i - 1)
                spread_v(i, 1)
                spread_v(i, 2)
                var_(i - 1)
                lora_in(i + 1, 0)
                lora_in(i + 1, 1)
                lora_in(i + 1, 2)
                spread_v(i, 3)
                unblock_rstd(i - 1)
                lora_in(i + 1, 3)
                spread_v(i, 4)
                lora_out(i + 1, 0)
                spread_v(i, 5)
                lora_out(i + 1, 1)
                lora_out(i + 1, 2)
                out_product(i - 1, 0)
                out_product(i - 1, 1)
                project_k(i + 1)
                lora_out(i + 1, 3)
                spread_v(i, 6)
                td_in_(i + 1)
                project_v(i + 1)
                tr2(i - 1)
                gather_half(i, 0)
                lora_out(i + 1, 4)
                spread_v(i, 7)
                td_out(i + 1)
                bonus_sum(i)
                ffn_k(i - 1, 0)
                ffn_k(i - 1, 1)
                project_r(i + 1)
                ffn_r(i - 1, 0)
                project_g(i + 1)
                ffn_r(i - 1, 1)
                ffn_v(i - 1, 0)
                ffn_v(i - 1, 1)
                gather_half(i, 1)
            spread_v(B - 1, 0)
            spread_v(B - 1, 1)
            mean_(B - 2)
            spread_v(B - 1, 2)
            spread_v(B - 1, 3)
            pe.wait_ge(r_ready, B)
            keep_clock(pa[2])
            spread_v(B - 1, 4)
            var_(B - 2)
            spread_v(B - 1, 5)
            spread_v(B - 1, 6)
            unblock_rstd(B - 2)
            spread_v(B - 1, 7)
            keep_clock(pa[2])
            out_product(B - 2, 0)
            out_product(B - 2, 1)
            bonus_sum(B - 1)
            keep_clock(pa[2])
            gather_half(B - 1, 0)
            gather_half(B - 1, 1)
            tr2(B - 2)
            mean_(B - 1)
            ffn_k(B - 2, 0)
            ffn_k(B - 2, 1)
            var_(B - 1)
            ffn_r(B - 2, 0)
            unblock_rstd(B - 1)
            ffn_r(B - 2, 1)
            ffn_v(B - 2, 0)
            ffn_v(B - 2, 1)
            out_product(B - 1, 0)
            out_product(B - 1, 1)
            tr2(B - 1)
            keep_clock(pa[2])
            keep_clock(pa[2])
            ffn_k(B - 1, 0)
            ffn_k(B - 1, 1)
            ffn_r(B - 1, 0)
            ffn_r(B - 1, 1)
            ffn_v(B - 1, 0)
            ffn_v(B - 1, 1)

PRE = "L0_xattn_"


def kernel(**inputs):
    import concourse.bacc as _bacc
    from concourse.bass_utils import run_bass_kernel_spmd as _run

    def get(name):
        return np.asarray(inputs[PRE + name])

    def halves(v):
        return v.reshape(HALVES, P).T

    def grouped(v):
        return v.reshape(H, Q, G).transpose(2, 0, 1).reshape(P, Q)

    def grouped_out(m):
        return m.reshape(H, Q, G, E).transpose(3, 1, 2, 0).reshape(E, E)

    maa = get("maa_stack").reshape(NMIX, E)
    cols = []
    for name in VECS:
        if name.startswith("gn_"):
            cols.append(grouped(get(name)))
        elif name[:3] == "maa" and name[3:].isdigit():
            cols.append(halves(maa[int(name[3:])]))
        else:
            cols.append(halves(get(name).reshape(E)))
    early, late = constants()
    w1, w2 = get("maa_w1"), get("maa_w2")
    w2_rows = np.zeros((P, NMIX, E), w2.dtype)
    for block in range(P // DM):
        for j in range(NMIX):
            if j == NMIX - 1 or j % 2 == block % 2:
                w2_rows[block * DM:(block + 1) * DM, j] = w2[j]
    arrays = {
        "x": np.asarray(inputs["x"]),
        "state": np.asarray(inputs["ctx_2048"]),
        "vecs": np.stack(cols, axis=1),
        "early": early,
        "late": late,
        "w1": np.concatenate([w1[:, 0:2 * DM]] * 2 + [w1[:, 2 * DM:4 * DM]] * 2 + [w1[:, 4 * DM:]] * 4, axis=1),
        "w2": w2_rows,
        "td1": np.concatenate([get("td_w1")] * 2, axis=1),
        "td2": np.concatenate([get("td_w2")] * 2, axis=0),
        "Wk": get("Wk").T,
        "Wr": get("Wr").T,
        "Wv": grouped_out(get("Wv")),
        "Wg": grouped_out(get("Wg")),
        "Wo": get("Wo").reshape(E, H, Q, G).transpose(2, 3, 1, 0).reshape(E, E),
        "Wfk": get("Wfk").T,
        "Wfr": get("Wfr").T,
        "Wfv": get("Wfv").T,
    }
    arrays = {f"in_{n}": np.ascontiguousarray(a) for n, a in arrays.items()}
    nc = _bacc.Bacc("TRN2", target_bir_lowering=False, num_devices=1)
    d = {n[3:]: nc.dram_tensor(n, a.shape, mybir.dt.from_np(a.dtype), kind="ExternalInput").ap()
         for n, a in arrays.items()}
    out = nc.dram_tensor("out_0", (B, L, E), F32, kind="ExternalOutput").ap()
    rwkv_block(nc, d["x"], d["state"], d["vecs"], d["early"], d["late"], d["w1"], d["w2"], d["td1"], d["td2"],
               {m: d[m] for m in MATS}, out)
    r = _run(nc, [arrays], core_ids=[0])
    return r.results[0]["out_0"]
```
